# Optimizing a Trainium2 kernel written in Bass

```python
import numpy as np
import jax
import jax.numpy as jnp

def _softmax(x, axis=-1):
    return jax.nn.softmax(x, axis=axis)

def _gelu(x):
    return jax.nn.gelu(x, approximate=True)

def _silu(x):
    return jax.nn.silu(x)

def _sigmoid(x):
    return jax.nn.sigmoid(x)

def _layernorm(x, axis=-1, eps=1e-05):
    m = jnp.mean(x, axis=axis, keepdims=True)
    v = jnp.var(x, axis=axis, keepdims=True)
    return (x - m) / jnp.sqrt(v + eps)

def _scatter_add(tgt, idx, src, axis=0):
    return tgt.at[idx].add(src)

def _segment_sum(src, seg, n):
    return jax.ops.segment_sum(src, seg, n)
kernel_name = 'mk_adaln_d1_jaxref_r4_bda720'

def setup_inputs(seed: int=0):
    np.random.seed(seed)
    _w = jnp.asarray

    def _L0_attn_setup():
        import jax, jax.numpy as jnp
        import numpy as np
        D_MODEL = 256
        N_HEADS = 32
        HEAD_DIM = D_MODEL // N_HEADS
        EPS = 1e-05
        key = jax.random.key(seed)
        ks = jax.random.split(key, 6)
        B, S = (2, 512)
        scale = 1.0 / np.sqrt(D_MODEL)
        return {'x': jax.random.normal(ks[0], (B, S, D_MODEL), dtype=jnp.float32), 'Wqkv_w': jax.random.normal(ks[1], (3 * D_MODEL, D_MODEL), dtype=jnp.float32) * scale, 'Wqkv_b': jax.random.normal(ks[2], (3 * D_MODEL,), dtype=jnp.float32) * 0.01, 'gn_w': jnp.ones((D_MODEL,), dtype=jnp.float32), 'gn_b': jnp.zeros((D_MODEL,), dtype=jnp.float32), 'out_w': jax.random.normal(ks[3], (D_MODEL, D_MODEL), dtype=jnp.float32) * scale, 'out_b': jax.random.normal(ks[4], (D_MODEL,), dtype=jnp.float32) * 0.01}
    _L0_attn_in = _L0_attn_setup()

    def _L0_ffn_setup():
        import jax, jax.numpy as jnp
        import numpy as np
        JITTER_EPS = 0.01

        def phi_routing(logits, jitter_eps=JITTER_EPS):
            m, sel = jax.lax.top_k(logits, 2)
            T, E = logits.shape
            m1 = m[:, :1]
            factor1 = jnp.maximum(jnp.abs(logits), m1)
            mask1 = (m1 - logits) / factor1 > 2.0 * jitter_eps
            p1 = jax.nn.softmax(jnp.where(mask1, -jnp.inf, logits), axis=-1)
            mult1 = jnp.take_along_axis(p1, sel[:, :1], axis=-1)
            m2 = m[:, 1:2]
            factor2 = jnp.maximum(jnp.abs(logits), m2)
            mask2 = (m2 - logits) / factor2 > 2.0 * jitter_eps
            drop_top1 = jnp.arange(E)[None, :] == sel[:, :1]
            p2 = jax.nn.softmax(jnp.where(mask2 | drop_top1, -jnp.inf, logits), axis=-1)
            mult2 = jnp.take_along_axis(p2, sel[:, 1:2], axis=-1)
            return (jnp.concatenate([mult1, mult2], axis=-1), sel)
        key = jax.random.key(seed)
        k = jax.random.split(key, 5)
        B, S, H, F, E = (1, 128, 256, 1024, 8)
        return {'hidden_states': jax.random.normal(k[0], (B, S, H), jnp.float32), 'gate_w': jax.random.normal(k[1], (E, H), jnp.float32) * 0.02, 'w1': jax.random.normal(k[2], (E, F, H), jnp.float32) * 0.02, 'w2': jax.random.normal(k[3], (E, H, F), jnp.float32) * 0.02, 'w3': jax.random.normal(k[4], (E, F, H), jnp.float32) * 0.02}
    _L0_ffn_in = _L0_ffn_setup()
    _L0_c = _w((lambda *s: np.random.randn(*s).astype(np.float32) * 0.05)(8, 256))
    _L0_wmod = _w((lambda *s: np.random.randn(*s).astype(np.float32) * 0.05)(256, 6 * 256) * 256 ** (-0.5))
    _d = {'L0_attn_x': _L0_attn_in['x'], 'L0_attn_Wqkv_w': _L0_attn_in['Wqkv_w'], 'L0_attn_Wqkv_b': _L0_attn_in['Wqkv_b'], 'L0_attn_gn_w': _L0_attn_in['gn_w'], 'L0_attn_gn_b': _L0_attn_in['gn_b'], 'L0_attn_out_w': _L0_attn_in['out_w'], 'L0_attn_out_b': _L0_attn_in['out_b'], 'L0_ffn_gate_w': _L0_ffn_in['gate_w'], 'L0_ffn_w1': _L0_ffn_in['w1'], 'L0_ffn_w2': _L0_ffn_in['w2'], 'L0_ffn_w3': _L0_ffn_in['w3'], 'L0_c': _L0_c, 'L0_wmod': _L0_wmod}
    _x0 = _d['L0_attn_x']
    _d['L0_attn_x'] = jax.random.normal(jax.random.fold_in(jax.random.key(seed), 1), (8, 512, 256), dtype=_x0.dtype)
    del _x0
    return _d

def reference(L0_attn_x, L0_attn_Wqkv_w, L0_attn_Wqkv_b, L0_attn_gn_w, L0_attn_gn_b, L0_attn_out_w, L0_attn_out_b, L0_ffn_gate_w, L0_ffn_w1, L0_ffn_w2, L0_ffn_w3, L0_c, L0_wmod):

    def _L0_attn_ref(x, Wqkv_w, Wqkv_b, gn_w, gn_b, out_w, out_b):
        import jax, jax.numpy as jnp
        import numpy as np
        D_MODEL = 256
        N_HEADS = 32
        HEAD_DIM = D_MODEL // N_HEADS
        EPS = 1e-05
        B, S, Dm = x.shape
        H, Dh = (N_HEADS, HEAD_DIM)
        qkv = x @ Wqkv_w.T + Wqkv_b
        qkv = qkv.reshape(B, S, 3, H, Dh)
        q, k, v = (qkv[:, :, 0], qkv[:, :, 1], qkv[:, :, 2])
        a = jnp.einsum('bthd,bshd->bhts', q, k)
        ctx = jnp.einsum('bhts,bshd->bthd', a, v)
        g = ctx.transpose(0, 2, 3, 1)
        mean = g.mean(axis=(2, 3), keepdims=True)
        var = ((g - mean) ** 2).mean(axis=(2, 3), keepdims=True)
        gh = (g - mean) * jax.lax.rsqrt(var + EPS)
        gh = gh * gn_w.reshape(H, Dh, 1) + gn_b.reshape(H, Dh, 1)
        ctx = gh.transpose(0, 3, 1, 2).reshape(B, S, Dm)
        return ctx @ out_w.T + out_b

    def _L0_ffn_ref(hidden_states, gate_w, w1, w2, w3):
        import jax, jax.numpy as jnp
        import numpy as np
        JITTER_EPS = 0.01

        def phi_routing(logits, jitter_eps=JITTER_EPS):
            m, sel = jax.lax.top_k(logits, 2)
            T, E = logits.shape
            m1 = m[:, :1]
            factor1 = jnp.maximum(jnp.abs(logits), m1)
            mask1 = (m1 - logits) / factor1 > 2.0 * jitter_eps
            p1 = jax.nn.softmax(jnp.where(mask1, -jnp.inf, logits), axis=-1)
            mult1 = jnp.take_along_axis(p1, sel[:, :1], axis=-1)
            m2 = m[:, 1:2]
            factor2 = jnp.maximum(jnp.abs(logits), m2)
            mask2 = (m2 - logits) / factor2 > 2.0 * jitter_eps
            drop_top1 = jnp.arange(E)[None, :] == sel[:, :1]
            p2 = jax.nn.softmax(jnp.where(mask2 | drop_top1, -jnp.inf, logits), axis=-1)
            mult2 = jnp.take_along_axis(p2, sel[:, 1:2], axis=-1)
            return (jnp.concatenate([mult1, mult2], axis=-1), sel)
        B, S, H = hidden_states.shape
        E = w1.shape[0]
        x = hidden_states.reshape(-1, H)
        logits = x @ gate_w.T
        routing_weights, selected = phi_routing(logits)
        T = x.shape[0]
        wte = jnp.zeros((T, E), x.dtype).at[jnp.arange(T)[:, None], selected].add(routing_weights)
        out = jnp.zeros_like(x)
        for e in range(E):
            h = jax.nn.silu(x @ w1[e].T) * (x @ w3[e].T)
            out = out + wte[:, e:e + 1] * (h @ w2[e].T)
        return out.reshape(B, S, H)
    x = L0_attn_x
    mod = (_silu(L0_c) @ L0_wmod).reshape(L0_c.shape[0], 6, 1, -1)
    sa, ca, ga, sb, cb, gb = (mod[:, 0], mod[:, 1], mod[:, 2], mod[:, 3], mod[:, 4], mod[:, 5])
    ga = (2 * (ga >= 0) - 1) * jnp.maximum(jnp.abs(ga), 0.25)
    gb = (2 * (gb >= 0) - 1) * jnp.maximum(jnp.abs(gb), 0.25)
    h = _layernorm(x, axis=-1) * (1 + ca) + sa
    x = x + ga * _L0_attn_ref(h, L0_attn_Wqkv_w, L0_attn_Wqkv_b, L0_attn_gn_w, L0_attn_gn_b, L0_attn_out_w, L0_attn_out_b)
    h = _layernorm(x, axis=-1) * (1 + cb) + sb
    x = x + gb * _L0_ffn_ref(h, L0_ffn_gate_w, L0_ffn_w1, L0_ffn_w2, L0_ffn_w3)
    return x

_drawn_inputs = setup_inputs


def setup_inputs(seed=0):
    import zlib

    import numpy as np

    out = dict(_drawn_inputs(seed))
    spreads = {'L0_attn_gn_w': (1.0, 0.2), 'L0_attn_gn_b': (0.0, 0.319)}
    factors = {'L0_attn_Wqkv_b': 8.0,
     'L0_attn_out_b': 8.0,
     'L0_ffn_gate_w': 5.666,
     'L0_ffn_w1': 4.988,
     'L0_ffn_w2': 4.931,
     'L0_ffn_w3': 4.94}
    for name, (base, spread) in spreads.items():
        noise = np.random.default_rng([zlib.crc32(name.encode()), seed]).standard_normal(out[name].shape)
        drawn = base * np.exp(spread * noise) if base else spread * noise
        out[name] = jnp.asarray(drawn.astype(out[name].dtype))
    for name, factor in factors.items():
        out[name] = (out[name] * factor).astype(out[name].dtype)
    return out
```

```python
from contextlib import ExitStack

import numpy as np

import concourse.bass as bass
from concourse import mybir
from concourse.alu_op_type import AluOpType as ALU

F32 = mybir.dt.float32
F32R = mybir.dt.float32r
BF16 = mybir.dt.bfloat16
I32 = mybir.dt.int32
U32 = mybir.dt.uint32
ACT = mybir.ActivationFunctionType
AX_X = mybir.AxisListType.X

P = 128
B, S, D = 8, 512, 256
E, F = 8, 1024
HEAD = 8
KH = D // P
NJ = S // P
BLK = 256
NT = BLK // P
NF = F // P
CAP = B * S + BLK
META = D
TOK, BAT = D + E, D + E + 1
RW = D + E + 2
NOROW = 1 << 20
WC = 1024
NCH = 3 * KH * F // WC
EPS = 1e-5
JITTER = 2.0 * 0.01


def constants():
    p = np.arange(P)
    parts = {
        "ident": np.eye(P),
        "mask": np.tile(p[:, None] // HEAD == p[None, :] // HEAD, (1, KH)),
        "avg": (p[:, None] // HEAD == p[None, :] // HEAD) / HEAD,
        "before": p[:, None] < p[None, :],
        "ones": np.ones((P, P)),
        "iota": np.tile(np.arange(E), (P, NJ)),
        "region": np.tile(np.arange(E) * CAP, (P, 1)),
        "padrow": p[:, None] + P * np.tile(np.arange(NT), E)[None, :],
        "token": np.stack([p[:, None] * NJ + np.arange(NJ)[None, :], np.zeros((P, NJ))], 2).reshape(P, 2 * NJ),
        "step": np.tile([S, 1], (P, NJ)),
        "half": np.full((P, NJ), -0.5),
    }
    at, where = 0, {}
    for name, a in parts.items():
        where[name] = (at, a.shape[1])
        at += a.shape[1]
    return np.concatenate([a.astype(np.float32) for a in parts.values()], 1), where


MODP = {"cT": KH * B, "ob": D, "wmod": KH * 6 * D}
ATTP = {"wqkv": KH * 3 * D, "bkv": 2 * D, "ow": KH * D, "gate": KH * E, "bq": KH, "gnw": KH, "gnb": KH}


def wait(eng, sem, value):
    if not (isinstance(value, int) and value <= 0):
        eng.wait_ge(sem, value)


def steps(eng, step, first, last, lo, hi):
    for i in range(first, lo):
        step(i, i % 2)
    with eng.Fori(0, (hi - lo + 1) // 2) as m:
        for s in range(2):
            step(m * 2 + (lo + s), (lo + s) % 2)
    for i in range(hi + 1, last + 1):
        step(i, i % 2)


def has(b):
    return not isinstance(b, int) or 0 <= b < B


def experts(eng, expert):
    with eng.Fori(0, E // 2 - 1) as m:
        for half in range(2):
            expert(m * 2 + half, half, True)
    for half in range(2):
        expert(E - 2 + half, half, half == 0)


def adaln_moe_kernel(nc, x, modp, attp, cst, we, out):
    _, CW = constants()
    ctx = ExitStack()
    with ctx:
        def sb(name, shape, dt=F32, stack=ctx):
            return stack.enter_context(nc.sbuf_tensor(name, shape, dt))

        def sem(name):
            return ctx.enter_context(nc.semaphore(name))

        modscr = nc.dram_tensor("modscr", [B, 4 * D], F32, kind="Internal").ap()
        gbscr = nc.dram_tensor("gbscr", [B, D], F32, kind="Internal").ap()
        xg = nc.dram_tensor("xg", [E * CAP, RW], F32, kind="Internal").ap()

        C = sb("C", [P, sum(n for _, n in CW.values())])
        whi = [sb("whi0", [P, NCH * WC], F32R), None]
        wlo = [sb("wlo0", [P, NCH * WC], F32R), None]
        raw = sb("raw", [P, NCH * WC])
        base = sb("base", [P, E])
        basei = sb("basei", [P, E])
        tabf = sb("tabf", [P, 4, E])
        tabi = sb("tabi", [P, E], I32)
        tab = sb("tab", [P, 2 * E], I32)
        padi = sb("padi", [P, E * NT], I32)
        padt = sb("padt", [P, RW])

        def c(name):
            a, n = CW[name]
            return C[:, a:a + n]

        att = ExitStack()
        X = sb("X", [P, B * NJ * D], stack=att)
        M1 = sb("M1", [P, sum(MODP.values())], stack=att)
        A1 = sb("A1", [P, sum(ATTP.values())], stack=att)
        sT = sb("sT", [P, KH, B], stack=att)
        sT1 = sb("sT1", [P, KH, B], stack=att)
        sT2 = sb("sT2", [P, KH, B], stack=att)
        modc = sb("modc", [P, 2, KH, B], stack=att)
        modr = sb("modr", [B, 5, D], stack=att)
        modt = sb("modt", [B, 2, 2, D], stack=att)
        modb = [sb(f"modb{q}", [P, 4, D], stack=att) for q in range(2)]
        xn = sb("xn", [P, NJ, D], stack=att)
        hT = sb("hT", [P, KH, S], stack=att)
        qT = sb("qT", [P, KH, S], stack=att)
        kv = sb("kv", [P, NJ, 2 * D], stack=att)
        bd = sb("bd", [P, KH, P], stack=att)
        gT = sb("gT", [P, KH, S], stack=att)
        owg = sb("owg", [P, KH, D], stack=att)
        h2 = [sb(f"h2{q}", [P, NJ, RW], stack=att) for q in range(2)]
        h2T = sb("h2T", [P, KH, S], stack=att)
        st1 = sb("st1", [P, NJ, 6], stack=att)
        mv1 = sb("mv1", [P, NJ, 2], stack=att)
        ve1 = sb("ve1", [P, NJ], stack=att)
        rs1 = sb("rs1", [P, NJ], stack=att)
        st2 = sb("st2", [P, NJ, 6], stack=att)
        mv2 = sb("mv2", [P, NJ, 2], stack=att)
        ve2 = sb("ve2", [P, NJ], stack=att)
        rs2 = sb("rs2", [P, NJ], stack=att)
        stc = sb("stc", [P, KH, 6], stack=att)
        mvc = sb("mvc", [P, KH, 2], stack=att)
        msq = sb("msq", [P, KH], stack=att)
        chst = sb("chst", [P, 2, KH], stack=att)
        gst = sb("gst", [P, 2, KH], stack=att)
        gnt = sb("gnt", [P, 6, KH], stack=att)
        gns = sb("gns", [P, 2, KH], stack=att)
        lg = sb("lg", [P, NJ, E], stack=att)
        alg = sb("alg", [P, NJ, E], stack=att)
        mx = sb("mx", [P, NJ, 8], stack=att)
        ix = sb("ix", [P, NJ, 8], U32, stack=att)
        ixf = sb("ixf", [P, 2, NJ], stack=att)
        dl = sb("dl", [P, 2, NJ, E], stack=att)
        fc = sb("fc", [P, 2, NJ, E], stack=att)
        un = sb("un", [P, 2, NJ, E], stack=att)
        dc = sb("dc", [P, 2, NJ, E], stack=att)
        ex = sb("ex", [P, 2, NJ, E], stack=att)
        eu = sb("eu", [P, 2, NJ, E], stack=att)
        oh = sb("oh", [P, 2, NJ, E], stack=att)
        sm = sb("sm", [P, 2 * NJ], stack=att)
        wk = sb("wk", [P, 2 * NJ], stack=att)
        wt = sb("wt", [P, 2, NJ, E], stack=att)
        mk = sb("mk", [P, NJ * E], BF16, stack=att)
        trib = sb("trib", [P, 2 * P], BF16, stack=att)
        tokf = sb("tokf", [P, 2 * NJ], stack=att)
        slf = sb("slf", [P, NJ, E], stack=att)
        ssel = sb("ssel", [P, 2, NJ, E], stack=att)
        srow = sb("srow", [P, 2 * NJ], stack=att)
        slot = [sb(f"slot{q}", [P, 2 * NJ], I32, stack=att) for q in range(2)]
        att.close()

        whi[1] = sb("whi1", [P, NCH * WC], F32R)
        wlo[1] = sb("wlo1", [P, NCH * WC], F32R)
        rows = sb("rows", [P, NT, RW])
        meta = sb("meta", [P, NT, RW - D])
        xhi = sb("xhi", [P, KH, BLK], F32R)
        xlo = sb("xlo", [P, KH, BLK], F32R)
        sg = sb("sg", [P, 2, BLK])
        hf = sb("hf", [P, NF, BLK])
        hhi = sb("hhi", [P, NF, BLK], F32R)
        hlo = sb("hlo", [P, NF, BLK], F32R)
        gbr = sb("gbr", [P, NT, D])
        ysb = sb("ysb", [P, NT, D])

        ps = [ctx.enter_context(nc.psum_tensor(f"ps{i}", [P, 512], F32)) for i in range(8)]

        c_ld, m_ld, a_ld = sem("c_ld"), sem("m_ld"), sem("a_ld")
        x_ld = [sem(f"x_ld{n}") for n in range(4)]
        raw_ld = sem("raw_ld")
        mc_exp, mc_sil, mc_ps, mc_v, mc_st, mb_ld = (sem(n) for n in ("mc_exp", "mc_sil", "mc_ps", "mc_v", "mc_st", "mb_ld"))
        ini, held = sem("ini"), sem("held")
        ln1_l, bn1, r1l, r1, xn_r = (sem(n) for n in ("ln1_l", "bn1", "r1l", "r1", "xn_r"))
        t1_ps, hT_r, q_ps, qT_r, kv_ps, kv_r, ktv_ps, bd_r = (
            sem(n) for n in ("t1_ps", "hT_r", "q_ps", "qT_r", "kv_ps", "kv_r", "ktv_ps", "bd_r"))
        c_ps, cs_l, cs_r, g_ps, g_cp, gn_l, gn_r, gT_r, owg_r = (
            sem(n) for n in ("c_ps", "cs_l", "cs_r", "g_ps", "g_cp", "gn_l", "gn_r", "gT_r", "owg_r"))
        gaob, o_ps, x1_r, x1_st = (sem(n) for n in ("gaob", "o_ps", "x1_r", "x1_st"))
        ln2_l, bn2, r2l, r2, xn2_r, md_l, h2_r = (sem(n) for n in ("ln2_l", "bn2", "r2l", "r2", "xn2_r", "md_l", "h2_r"))
        t2_ps, h2T_r, l_ps, ro_l, dc_r, ex_r, mk_r, r_ps, rp_l, sl_r, scat, sc_r = (
            sem(n) for n in ("t2_ps", "h2T_r", "l_ps", "ro_l", "dc_r", "ex_r", "mk_r", "r_ps", "rp_l", "sl_r", "scat", "sc_r"))
        wp_h, w_r0, w_r1 = sem("wp_h"), sem("w_r0"), sem("w_r1")
        w_r = [w_r0, w_r1]
        tb_l, tab_r, pad_r, pad_st = (sem(n) for n in ("tb_l", "tab_r", "pad_r", "pad_st"))
        row_ld, tp_ps, xh_r, xT_r, gu_ps, sg_r, hf_r, hi_r, hs_r = (
            sem(n) for n in ("row_ld", "tp_ps", "xh_r", "xT_r", "gu_ps", "sg_r", "hf_r", "hi_r", "hs_r"))
        y_ps, y_r, gb_ld, add_st, mt_r = (sem(n) for n in ("y_ps", "y_r", "gb_ld", "add_st", "mt_r"))

        def part(tile, table, name):
            at = 0
            for n, w in table.items():
                if n == name:
                    return tile[:, at:at + w]
                at += w
            raise KeyError(name)

        cT = part(M1, MODP, "cT").rearrange("p (k b) -> p k b", k=KH)
        ob = part(M1, MODP, "ob")
        wmod = part(M1, MODP, "wmod").rearrange("p (k n) -> p k n", k=KH)
        wqkv = part(A1, ATTP, "wqkv").rearrange("p (k n) -> p k n", k=KH)
        bkv = part(A1, ATTP, "bkv")
        ow = part(A1, ATTP, "ow").rearrange("p (k n) -> p k n", k=KH)
        gate = part(A1, ATTP, "gate").rearrange("p (k n) -> p k n", k=KH)
        bq, gnw, gnb = (part(A1, ATTP, n) for n in ("bq", "gnw", "gnb"))
        ident = c("ident")

        def xb(b, off=0, n=NJ * D):
            return X[:, bass.ds(b * (NJ * D) + off, n)]

        def split(ap, **kw):
            return ap.rearrange("p (a b) -> p a b", **kw)

        def flat(tile):
            return tile[:, :, :, :].rearrange("p a b c -> p (a b c)")

        def hold(eng, s, value):
            if not (isinstance(value, int) and value <= 0):
                eng.wait_ge(s, value)
                eng.sem_inc(held, 1)

        def linker(eng, s, b, per, wait_ge=lambda eng, s, v: eng.wait_ge(s, v)):
            n = [0]

            def link(ins):
                n[0] += 1
                assert n[0] <= per
                ins.then_inc(s, 1)
                wait_ge(eng, s, b * per + n[0])
            return link

        block = ctx.enter_context(nc.Block())

        @block.sync
        def _(sp):
            xv = x.rearrange("(b p j) d -> p b (j d)", p=P, j=NJ)
            Xv = X[:, :].rearrange("p (b n) -> p b n", b=B)
            ov = out.rearrange("(b p j) d -> b p (j d)", p=P, j=NJ)
            sp.dma_start(M1[:, :], modp).then_inc(m_ld, 16)
            sp.dma_start(Xv[:, 0:1, :], xv[:, 0:1, :]).then_inc(x_ld[0], 16)
            sp.dma_start(C[:, :], cst).then_inc(c_ld, 16)
            sp.dma_start(A1[:, :], attp).then_inc(a_ld, 16)
            for n, (lo, hi) in ((1, (1, 2)), (2, (2, 3)), (3, (3, B))):
                sp.dma_start(Xv[:, lo:hi, :], xv[:, lo:hi, :]).then_inc(x_ld[n], 16)
            sp.wait_ge(mc_v, 12)
            sp.dma_start(modscr, modr[:, 0:4, :]).then_inc(mc_st, 16)
            sp.dma_start(gbscr, modr[:, 4, :]).then_inc(mc_st, 16)
            sp.wait_ge(mc_st, 32)

            def load_mod(b, q):
                sp.dma_start(modb[q][:, :, :].rearrange("p a n -> p (a n)"),
                             modscr[bass.ds(b, 1), :].broadcast_to([P, 4 * D])).then_inc(mb_ld, 16)

            load_mod(0, 0)
            sp.wait_ge(mb_ld, 16)
            load_mod(1, 1)

            def store(b, q):
                hold(sp, x1_r, b * 2 + 2)
                sp.dma_start(ov[bass.ds(b, 1), :, :].rearrange("o p n -> (o p) n"), xb(b)).then_inc(x1_st, 16)

            def step(b, q):
                hold(sp, mb_ld, b * 16 + 32)
                hold(sp, h2_r, b + 1)
                load_mod(b + 2, q)
                store(b, q)

            steps(sp, step, 0, B - 3, 0, B - 3)
            store(B - 2, 0)
            store(B - 1, 1)

            sp.wait_ge(scat, 128 * B)
            sp.wait_ge(pad_st, 16 * NT * E)
            sp.wait_ge(tab_r, 1)

            def load_rows(first, g):
                hold(sp, tp_ps, g + 1)
                hold(sp, mt_r, g + 1)
                sp.dma_start(rows[:, :, :], xg[bass.ds(first, BLK), :].rearrange("(p t) d -> p t d", t=NT))\
                  .then_inc(row_ld, 16)

            def expert(e, half, more):
                n = sp.value_load(tab[0:1, bass.ds(e, 1)], min_val=1, max_val=B * S // BLK)
                g0 = sp.value_load(tab[0:1, bass.ds(e + E, 1)], min_val=0, max_val=2 * B * S)
                with sp.Fori(0, n) as k:
                    load_rows(e * CAP + k * BLK, g0 + k)

            experts(sp, expert)
            n = sp.value_load(tab[0:1, E - 1:E], min_val=1, max_val=B * S // BLK)
            g0 = sp.value_load(tab[0:1, 2 * E - 1:2 * E], min_val=0, max_val=2 * B * S)
            load_rows(0, g0 + n)
            hold(sp, row_ld, (g0 + n) * 16 + 16)
            sp.wait_ge(x1_st, 16 * B)
            hold(sp, add_st, (g0 + n) * 32)
            hold(sp, gb_ld, (g0 + n) * 32 + 32)

        @block.tensor
        def _(pe):
            pe.wait_ge(m_ld, 16)
            pe.wait_ge(mc_sil, 3)
            for n, ch in enumerate((1, 0)):
                for h in range(KH):
                    for k in range(KH):
                        pe.matmul(ps[0][:, (n * KH + h) * B:(n * KH + h + 1) * B],
                                  wmod[:, k, ch * D + h * P:ch * D + (h + 1) * P], sT[:, k, :],
                                  start=(k == 0), stop=(k == KH - 1))
            for n, ch in enumerate((2, 4, 3, 5)):
                for k in range(KH):
                    mm = pe.matmul(ps[1 + n // 2][0:B, n % 2 * D:(n % 2 + 1) * D], sT[:, k, :],
                                   wmod[:, k, ch * D:(ch + 1) * D], start=(k == 0), stop=(k == KH - 1))
            mm.then_inc(mc_ps, 1)
            pe.wait_ge(c_ld, 16)
            pe.wait_ge(a_ld, 16)
            pe.wait_ge(mc_v, 12)
            pe.wait_ge(ini, 2)

            def step(i, q):
                cur, nxt, prv = has(i), has(i + 1), has(i - 1)
                if cur:
                    pe.wait_ge(bd_r, i + 1)
                    pe.wait_ge(qT_r, i * 2 + 2)
                    wait(pe, x1_r, i * 2)
                    for h in range(KH):
                        pe.matmul(ps[2 + h][:, :], bd[:, h, :], qT[:, h, :], start=True, stop=True).then_inc(c_ps, 1)
                if nxt:
                    pe.wait_ge(xn_r, i + 2)
                    for h in range(KH):
                        for j in range(NJ):
                            mm = pe.transpose(ps[h][:, j * P:(j + 1) * P], xn[:, j, h * P:(h + 1) * P], ident)
                        mm.then_inc(t1_ps, 1)
                    for m in range(KH):
                        for k in range(KH):
                            pe.wait_ge(hT_r, (i + 1) * 2 + k + 1)
                            mm = pe.matmul(ps[4 + m][:, :], wqkv[:, k, m * P:(m + 1) * P], hT[:, k, :],
                                           start=(k == 0), stop=(k == KH - 1))
                        mm.then_inc(q_ps, 1)
                if cur:
                    pe.wait_ge(cs_r, i + 1)
                    pe.matmul(ps[6][:, 0:2 * KH], c("avg"), chst[:, :, :].rearrange("p a b -> p (a b)"),
                              start=True, stop=True).then_inc(g_ps, 1)
                if nxt:
                    for j in range(NJ):
                        if j < 2:
                            pe.wait_ge(qT_r, (i + 1) * 2 + j + 1)
                        else:
                            pe.wait_ge(kv_r, (i + 1) * NJ + j - 1)
                        for k in range(KH):
                            mm = pe.matmul(ps[4 + j % 2][:, :], hT[:, k, j * P:(j + 1) * P], wqkv[:, k, D:3 * D],
                                           start=(k == 0), stop=(k == KH - 1))
                        mm.then_inc(kv_ps, 1)
                if prv:
                    pe.wait_ge(h2_r, i)
                    for h in range(KH):
                        for j in range(NJ):
                            mm = pe.transpose(ps[h][:, j * P:(j + 1) * P], h2[1 - q][:, j, h * P:(h + 1) * P], ident)
                        mm.then_inc(t2_ps, 1)
                    pe.wait_ge(h2T_r, i * 2)
                    for j in range(NJ):
                        for k in range(KH):
                            mm = pe.matmul(ps[7][:, j * E:(j + 1) * E], h2T[:, k, j * P:(j + 1) * P], gate[:, k, :],
                                           start=(k == 0), stop=(k == KH - 1))
                    mm.then_inc(l_ps, 1)
                if nxt:
                    wait(pe, g_cp, i + 1)
                    pe.wait_ge(kv_r, (i + 2) * NJ)
                    for h in range(KH):
                        for j in range(NJ):
                            mm = pe.matmul(ps[6][:, h * P:(h + 1) * P], kv[:, j, h * P:(h + 1) * P],
                                           kv[:, j, D + h * P:D + (h + 1) * P], start=(j == 0), stop=(j == NJ - 1))
                    mm.then_inc(ktv_ps, 1)
                if cur:
                    pe.wait_ge(gT_r, i * 2 + 2)
                    pe.wait_ge(owg_r, i + 1)
                    for j in range(NJ):
                        for k in range(KH):
                            mm = pe.matmul(ps[2 + j // 2][:, j % 2 * D:(j % 2 + 1) * D], gT[:, k, j * P:(j + 1) * P],
                                           owg[:, k, :], start=(k == 0), stop=(k == KH - 1))
                        if j % 2:
                            mm.then_inc(o_ps, 1)
                if prv:
                    pe.wait_ge(mk_r, i)
                    for j in range(NJ + 1):
                        o = ps[7][:, 64 + j * E:64 + (j + 1) * E]
                        for n in range(min(j + 1, NJ)):
                            mm = pe.matmul(o, trib[:, P:2 * P] if n < j else trib[:, 0:P], mk[:, n * E:(n + 1) * E],
                                           start=(n == 0), stop=(n == min(j, NJ - 1)))
                    mm.then_inc(r_ps, 1)

            steps(pe, step, -1, B, 1, B - 2)

            def turn(g):
                pe.wait_ge(row_ld, g * 16 + 16)
                for k in range(KH):
                    for t in range(NT):
                        mm = pe.transpose(ps[7][:, k * BLK + t * P:k * BLK + (t + 1) * P], rows[:, t, k * P:(k + 1) * P],
                                          ident)
                mm.then_inc(tp_ps, 1)

            def expert(e, half, more):
                hi, lo = whi[half], wlo[half]
                n = pe.value_load(tab[0:1, bass.ds(e, 1)], min_val=1, max_val=B * S // BLK)
                g0 = pe.value_load(tab[0:1, bass.ds(e + E, 1)], min_val=0, max_val=2 * B * S)
                hold(pe, w_r[half], (e - half) // 2 + 1)

                def up(g, f):
                    pe.wait_ge(hf_r, g * NF + f + 1)
                    for n_, o in enumerate((0, BLK)):
                        for k in range(KH):
                            at = (n_ * KH + k) * F + f * P
                            for a, b_ in ((hi, xhi), (lo, xhi), (hi, xlo)):
                                mm = pe.matmul(ps[f % 4][:, o:o + BLK], a[:, at:at + P], b_[:, k, :],
                                               start=(k == 0 and a is hi and b_ is xhi),
                                               stop=(k == KH - 1 and b_ is xlo))
                    mm.then_inc(gu_ps, 1)

                def down(g, f):
                    pe.wait_ge(hs_r, g * NF + f + 1)
                    if f == 0:
                        pe.wait_ge(y_r, g + 1)
                    at = (2 * KH * F) + f * D
                    for t in range(NT):
                        for a, b_ in ((hhi, hi), (hlo, hi), (hhi, lo)):
                            mm = pe.matmul(ps[4 + t][:, 0:D], a[:, f, t * P:(t + 1) * P], b_[:, at:at + D],
                                           start=(f == 0 and a is hhi and b_ is hi),
                                           stop=(f == NF - 1 and b_ is lo))
                    if f == NF - 1:
                        mm.then_inc(y_ps, 1)

                with pe.Fori(0, n) as k_:
                    g = g0 + k_
                    pe.wait_ge(xT_r, g + 1)
                    for f in range(NF):
                        up(g, f)
                        if f == NF - 1:
                            turn(g + 1)
                        if f >= 2:
                            down(g, f - 2)
                    down(g, NF - 2)
                    down(g, NF - 1)

            pe.wait_ge(sl_r, B)
            pe.wait_ge(tab_r, 1)
            turn(0)
            experts(pe, expert)

        @block.scalar
        def _(act):
            act.wait_ge(m_ld, 16)
            act.activation(sT1[:, :, :], cT, ACT.Exp, scale=-1.0).then_inc(mc_exp, 1)
            act.dma_start(raw[:, :].rearrange("p (c n) -> p c n", c=NCH),
                          we[0].rearrange("c p n -> p c n")).then_inc(raw_ld, 16)
            act.wait_ge(mc_v, 12)
            act.wait_ge(a_ld, 16)

            def step(i, q):
                cur, nxt, prv = has(i), has(i + 1), has(i - 1)
                if nxt:
                    for h in range(KH):
                        act.wait_ge(t1_ps, (i + 1) * 2 + h + 1)
                        act.activation(hT[:, h, :], ps[h][:, :], ACT.Identity, bias=modc[:, 1, h, bass.ds(i + 1, 1)],
                                       scale=modc[:, 0, h, bass.ds(i + 1, 1)]).then_inc(hT_r, 1)
                    for m in range(KH):
                        act.wait_ge(q_ps, (i + 1) * 2 + m + 1)
                        act.activation(qT[:, m, :], ps[4 + m][:, :], ACT.Identity, bias=bq[:, m:m + 1]).then_inc(qT_r, 1)
                if cur:
                    act.wait_ge(gn_r, i + 1)
                    for h in range(KH):
                        act.activation(gT[:, h, :], ps[2 + h][:, :], ACT.Identity, bias=gns[:, 1, h:h + 1],
                                       scale=gns[:, 0, h:h + 1]).then_inc(gT_r, 1)
                if prv:
                    for h in range(KH):
                        act.wait_ge(t2_ps, (i - 1) * 2 + h + 1)
                        act.activation(h2T[:, h, :], ps[h][:, :], ACT.Copy).then_inc(h2T_r, 1)
                    act.wait_ge(dc_r, i)
                    act.activation(flat(ex), flat(dc), ACT.Exp, scale=-1.0).then_inc(ex_r, 1)

            steps(act, step, -1, B, 1, B - 2)

            act.wait_ge(sl_r, B)
            act.wait_ge(tab_r, 1)

            def turned(g):
                act.wait_ge(tp_ps, g + 2)
                act.activation(xhi[:, :, :].rearrange("p k n -> p (k n)"), ps[7][:, :], ACT.Copy).then_inc(xh_r, 1)

            turned(0)

            def expert(e, half, more):
                n = act.value_load(tab[0:1, bass.ds(e, 1)], min_val=1, max_val=B * S // BLK)
                g0 = act.value_load(tab[0:1, bass.ds(e + E, 1)], min_val=0, max_val=2 * B * S)
                if more:
                    hold(act, w_r[half], (e - half) // 2 + 1)
                    act.dma_start(raw[:, :].rearrange("p (c n) -> p c n", c=NCH),
                                  we[bass.ds(e + 1, 1)].rearrange("o c p n -> p (o c) n")).then_inc(raw_ld, 16)

                def high(g, f):
                    act.wait_ge(hf_r, g * NF + f + 1 + 4)
                    act.activation(hhi[:, f, :], hf[:, f, :], ACT.Copy).then_inc(hi_r, 1)

                with act.Fori(0, n) as k:
                    g = g0 + k
                    for f in range(NF):
                        act.wait_ge(gu_ps, g * NF + f + 1)
                        act.wait_ge(hf_r, g * NF + f + 3)
                        act.activation(sg[:, f % 2, :], ps[f % 4][:, 0:BLK], ACT.Silu).then_inc(sg_r, 1)
                        if f:
                            high(g, f - 1)
                    turned(g + 1)
                    high(g, NF - 1)

            experts(act, expert)

        @block.vector
        def _(dve):
            dve.wait_ge(mc_exp, 1)
            dve.tensor_scalar(sT2[:, :, :], sT1[:, :, :], 1.0, None, ALU.add).then_inc(mc_sil, 1)
            dve.wait_ge(mc_sil, 1)
            dve.reciprocal(sT1[:, :, :], sT2[:, :, :]).then_inc(mc_sil, 1)
            dve.wait_ge(mc_sil, 2)
            dve.tensor_tensor(sT[:, :, :], sT1[:, :, :], cT, ALU.mult).then_inc(mc_sil, 1)

            def layer_stats(b, src, stt_, mv, l, out_sem):
                for j in range(NJ):
                    ins = dve.bn_stats(stt_[:, j, :], src(b, j * D, D))
                ins.then_inc(l, 1)
                hold(dve, l, b + 1)
                for j in range(NJ):
                    ins = dve.bn_aggr(mv[:, j, :], stt_[:, j, :])
                ins.then_inc(out_sem, 1)

            def first_stats(b):
                if isinstance(b, int):
                    dve.wait_ge(x_ld[min(b, 3)], 16)
                layer_stats(b, xb, st1, mv1, ln1_l, bn1)

            def first_norm(b):
                dve.wait_ge(r1, b + 1)
                wait(dve, t1_ps, b * 2)
                for j in range(NJ):
                    ins = dve.tensor_scalar(xn[:, j, :], xb(b, j * D, D), mv1[:, j, 0:1], rs1[:, j:j + 1],
                                            ALU.subtract, ALU.mult)
                ins.then_inc(xn_r, 1)

            first_stats(0)
            dve.wait_ge(mc_ps, 1)
            dve.tensor_scalar(modc[:, 0, :, :], split(ps[0][:, 0:KH * B], a=KH), 1.0, None, ALU.add).then_inc(mc_v, 1)
            dve.tensor_copy(modc[:, 1, :, :], split(ps[0][:, KH * B:2 * KH * B], a=KH)).then_inc(mc_v, 1)
            g2 = (ps[1][0:B, 0:D], ps[2][0:B, D:2 * D])
            for n in range(2):
                dve.tensor_scalar(modt[:, n, 0, :], g2[n], 0.0, None, ALU.is_ge).then_inc(mc_v, 1)
                dve.tensor_scalar(modt[:, n, 1, :], g2[n], -1.0, None, ALU.mult).then_inc(mc_v, 1)
            dve.wait_ge(mc_v, 6)
            for n in range(2):
                dve.tensor_scalar(modt[:, n, 0, :], modt[:, n, 0, :], 2.0, -1.0, ALU.mult, ALU.add)
                dve.scalar_tensor_tensor(modt[:, n, 1, :], modt[:, n, 1, :], 0.25, g2[n], ALU.max, ALU.max)\
                   .then_inc(mc_v, 1)
            dve.wait_ge(mc_v, 8)
            dve.tensor_tensor(modr[:, 0, :], modt[:, 0, 0, :], modt[:, 0, 1, :], ALU.mult).then_inc(mc_v, 1)
            dve.tensor_tensor(modr[:, 4, :], modt[:, 1, 0, :], modt[:, 1, 1, :], ALU.mult)
            dve.tensor_scalar(modr[:, 2, :], ps[1][0:B, D:2 * D], 1.0, None, ALU.add).then_inc(mc_v, 1)
            dve.tensor_copy(modr[:, 3, :], ps[2][0:B, 0:D]).then_inc(mc_v, 1)
            dve.wait_ge(mc_v, 9)
            dve.tensor_tensor(modr[:, 1, :], modr[:, 0, :], ob[0:B, :], ALU.mult).then_inc(mc_v, 1)
            dve.wait_ge(c_ld, 16)
            dve.tensor_copy(trib[:, :], C[:, CW["before"][0]:CW["before"][0] + 2 * P]).then_inc(ini, 1)
            dve.tensor_copy(base[:, :], c("region")).then_inc(ini, 1)
            dve.tensor_copy(tokf[:, :], c("token")).then_inc(ini, 1)
            dve.wait_ge(ini, 3)
            dve.wait_ge(a_ld, 16)

            def context_stats(i):
                link = linker(dve, cs_l, i, 3, hold)
                for h in range(KH):
                    dve.wait_ge(c_ps, i * 2 + h + 1)
                    ins = dve.bn_stats(stc[:, h, :], ps[2 + h][:, :])
                link(ins)
                for h in range(KH):
                    ins = dve.bn_aggr(mvc[:, h, :], stc[:, h, :])
                link(ins)
                dve.tensor_copy(chst[:, 0, :], mvc[:, :, 0])
                link(dve.tensor_tensor(msq[:, :], mvc[:, :, 0], mvc[:, :, 0], ALU.mult))
                dve.tensor_tensor(chst[:, 1, :], msq[:, :], mvc[:, :, 1], ALU.add).then_inc(cs_r, 1)

            def keep_kv(b, j):
                dve.wait_ge(kv_ps, b * NJ + j + 1)
                dve.tensor_tensor(kv[:, j, :], ps[4 + j % 2][:, :], bkv, ALU.add).then_inc(kv_r, 1)

            def routing(b, q):
                link = linker(dve, ro_l, b, 5)
                dve.wait_ge(l_ps, b + 1)
                link(dve.tensor_copy(lg[:, :, :], split(ps[7][:, 0:NJ * E], a=NJ)))
                dve.scalar_tensor_tensor(alg[:, :, :], lg[:, :, :], -1.0, lg[:, :, :], ALU.mult, ALU.max)
                for j in range(NJ):
                    ins = dve.max(mx[:, j, :], lg[:, j, :])
                link(ins)
                for k in range(2):
                    best = mx[:, :, k:k + 1].broadcast_to([P, NJ, E])
                    dve.tensor_tensor(dl[:, k, :, :], best, lg[:, :, :], ALU.subtract)
                    dve.tensor_tensor(fc[:, k, :, :], best, alg[:, :, :], ALU.max)
                for j in range(NJ):
                    ins = dve.max_index(ix[:, j, :], mx[:, j, :], lg[:, j, :])
                link(ins)
                dve.tensor_copy(ixf[:, :, :], ix[:, :, 0:2].rearrange("p j k -> p k j"))
                dve.tensor_scalar(flat(dc), flat(dl), 0.0, None, ALU.max).then_inc(dc_r, 1)
                link(dve.scalar_tensor_tensor(flat(un), flat(fc), JITTER, flat(dl), ALU.mult, ALU.is_ge))
                for k in range(2):
                    ins = dve.tensor_tensor(oh[:, k, :, :], split(c("iota"), a=NJ),
                                            ixf[:, k, :].rearrange("p (j o) -> p j o", o=1).broadcast_to([P, NJ, E]),
                                            ALU.is_equal)
                link(ins)
                dve.scalar_tensor_tensor(un[:, 1, :, :], oh[:, 0, :, :], 0.5, un[:, 1, :, :], ALU.is_lt, ALU.mult)
                dve.tensor_tensor(split(mk[:, :], a=NJ), oh[:, 0, :, :], oh[:, 1, :, :], ALU.add).then_inc(mk_r, 1)

            def routed(b, q):
                link = linker(dve, rp_l, b, 4)
                dve.wait_ge(ex_r, b + 1)
                dve.wait_ge(mk_r, b + 1)
                dve.wait_ge(r_ps, b + 1)
                dve.tensor_tensor(flat(eu), flat(ex), flat(un), ALU.mult)
                link(dve.tensor_tensor(slf[:, :, :], split(ps[7][:, 64:64 + NJ * E], a=NJ),
                                       base[:, :].rearrange("p (o e) -> p o e", o=1).broadcast_to([P, NJ, E]), ALU.add))
                dve.tensor_reduce(sm[:, :], eu[:, :, :, :].rearrange("p a b c -> p (a b) c"), AX_X, ALU.add)
                for k in range(2):
                    dve.tensor_tensor(ssel[:, k, :, :], oh[:, k, :, :], slf[:, :, :], ALU.mult)
                dve.tensor_copy(h2[q][:, :, TOK:TOK + 2].bitcast(I32), split(tokf[:, :], a=NJ))
                link(dve.tensor_tensor(base[:, :], base[:, :], ps[7][:, 64 + NJ * E:64 + (NJ + 1) * E], ALU.add))
                dve.reciprocal(wk[:, :], sm[:, :])
                dve.tensor_tensor(tokf[:, :], tokf[:, :], c("step"), ALU.add)
                link(dve.tensor_reduce(srow[:, :], ssel[:, :, :, :].rearrange("p a b c -> p (a b) c"), AX_X, ALU.add))
                dve.tensor_copy(slot[q][:, :], srow[:, :])
                link(dve.tensor_tensor(wt[:, :, :, :].rearrange("p a b c -> p (a b) c"),
                                       oh[:, :, :, :].rearrange("p a b c -> p (a b) c"),
                                       wk[:, :].rearrange("p (n o) -> p n o", o=1).broadcast_to([P, 2 * NJ, E]), ALU.mult))
                dve.tensor_tensor(h2[q][:, :, META:META + E], wt[:, 0, :, :], wt[:, 1, :, :], ALU.add).then_inc(sl_r, 1)

            def step(i, q):
                cur, nxt, prv, nx2 = has(i), has(i + 1), has(i - 1), has(i + 2)
                if cur:
                    context_stats(i)
                if prv:
                    layer_stats(i - 1, xb, st2, mv2, ln2_l, bn2)
                if cur:
                    dve.wait_ge(g_ps, i + 1)
                    dve.tensor_copy(gst[:, :, :].rearrange("p a b -> p (a b)"), ps[6][:, 0:2 * KH]).then_inc(g_cp, 1)
                if nx2:
                    first_stats(i + 2)
                if prv:
                    dve.wait_ge(r2, i)
                    dve.wait_ge(sc_r, i)
                    for j in range(NJ):
                        ins = dve.tensor_scalar(h2[1 - q][:, j, 0:D], xb(i - 1, j * D, D), mv2[:, j, 0:1],
                                                rs2[:, j:j + 1], ALU.subtract, ALU.mult)
                    ins.then_inc(xn2_r, 1)
                if nxt:
                    keep_kv(i + 1, 0)
                    keep_kv(i + 1, 1)
                if cur:
                    dve.wait_ge(mb_ld, i * 16 + 16)
                    dve.tensor_tensor(split(xb(i), a=NJ), split(xb(i), a=NJ),
                                      modb[q][:, 1:2, :].broadcast_to([P, NJ, D]), ALU.add).then_inc(gaob, 1)
                if nx2:
                    first_norm(i + 2)
                if nxt:
                    keep_kv(i + 1, 2)
                    keep_kv(i + 1, 3)
                if prv:
                    routing(i - 1, 1 - q)
                if nxt:
                    dve.wait_ge(ktv_ps, i + 2)
                    dve.tensor_tensor(bd[:, :, :].rearrange("p a b -> p (a b)"), ps[6][:, 0:KH * P], c("mask"), ALU.mult)\
                       .then_inc(bd_r, 1)
                if cur:
                    dve.wait_ge(gaob, i + 1)
                    for n in range(2):
                        dve.wait_ge(o_ps, i * 2 + n + 1)
                        dve.tensor_tensor(xb(i, n * 2 * D, 2 * D), ps[2 + n][:, :], xb(i, n * 2 * D, 2 * D), ALU.add)\
                           .then_inc(x1_r, 1)
                    dve.wait_ge(x1_r, i * 2 + 2)
                if prv:
                    routed(i - 1, 1 - q)

            first_norm(0)
            steps(dve, step, -1, B, 1, B - 4)

            n_tab = [0]

            def tlink(ins):
                n_tab[0] += 1
                ins.then_inc(tb_l, 1)
                dve.wait_ge(tb_l, n_tab[0])

            dve.tensor_tensor(padi[:, :].rearrange("p (e t) -> p e t", t=NT),
                              base[:, :].rearrange("p (e o) -> p e o", o=1).broadcast_to([P, E, NT]),
                              c("padrow").rearrange("p (e t) -> p e t", t=NT), ALU.add)
            dve.memset(padt[:, :], 0.0)
            tlink(dve.tensor_tensor(tabf[:, 0, :], base[:, :], c("region"), ALU.subtract))
            dve.memset(padt[:, TOK:TOK + 1].bitcast(I32), NOROW).then_inc(pad_r, 1)
            tlink(dve.tensor_scalar(tabf[:, 1, :], tabf[:, 0, :], float(BLK - 1), None, ALU.add))
            tlink(dve.tensor_copy(tabi[:, :], tabf[:, 1, :]))
            tlink(dve.tensor_scalar(tab[:, 0:E], tabi[:, :], BLK.bit_length() - 1, None, ALU.logical_shift_right))
            tlink(dve.tensor_copy(tabf[:, 2, :], tab[:, 0:E]))
            tlink(dve.tensor_scalar(tabf[:, 3, :], tabf[:, 2, :], 1.0, None, ALU.max))
            tlink(dve.tensor_tensor_scan(tabf[:, 0, :], c("ones")[:, 0:E], tabf[:, 3, :], 0.0, ALU.mult, ALU.add))
            tlink(dve.tensor_tensor(tabf[:, 1, :], tabf[:, 0, :], tabf[:, 3, :], ALU.subtract))
            dve.tensor_copy(tab[:, 0:E], tabf[:, 3, :])
            dve.tensor_copy(tab[:, E:2 * E], tabf[:, 1, :]).then_inc(tab_r, 1)
            dve.wait_ge(tab_r, 1)

            def turned(g):
                dve.wait_ge(xh_r, g + 1)
                dve.tensor_tensor(xlo[:, :, :].rearrange("p k n -> p (k n)"), ps[7][:, :],
                                  xhi[:, :, :].rearrange("p k n -> p (k n)").bitcast(F32), ALU.subtract).then_inc(xT_r, 1)

            turned(0)

            def expert(e, half, more):
                n = dve.value_load(tab[0:1, bass.ds(e, 1)], min_val=1, max_val=B * S // BLK)
                g0 = dve.value_load(tab[0:1, bass.ds(e + E, 1)], min_val=0, max_val=2 * B * S)

                def low(g, f):
                    dve.wait_ge(hi_r, g * NF + f + 1)
                    dve.tensor_tensor(hlo[:, f, :], hf[:, f, :], hhi[:, f, :].bitcast(F32), ALU.subtract)\
                       .then_inc(hs_r, 1)

                with dve.Fori(0, n) as k:
                    g = g0 + k
                    for f in range(NF):
                        dve.wait_ge(sg_r, g * NF + f + 1)
                        dve.tensor_tensor(hf[:, f, :], ps[f % 4][:, BLK:2 * BLK], sg[:, f % 2, :], ALU.mult)\
                           .then_inc(hf_r, 1)
                        if f:
                            low(g, f - 1)
                    turned(g + 1)
                    low(g, NF - 1)
                    dve.wait_ge(gb_ld, g * 32 + 32)
                    dve.wait_ge(y_ps, g + 2)
                    for t in range(NT):
                        ins = dve.scalar_tensor_tensor(ysb[:, t, :], ps[4 + t][:, 0:D], meta[:, t, bass.ds(e, 1)],
                                                       gbr[:, t, :], ALU.mult, ALU.mult)
                    ins.then_inc(y_r, 1)

            experts(dve, expert)

        @block.gpsimd
        def _(pool):
            pool.memset(basei[:, 0:1], 0.0).then_inc(hf_r, 4)
            pool.memset(basei[:, 1:2], 0.0).then_inc(y_r, 1)
            pool.memset(basei[:, 2:3], 0.0).then_inc(y_ps, 1)
            pool.memset(basei[:, 3:4], 0.0).then_inc(tp_ps, 1)
            pool.memset(basei[:, 4:5], 0.0).then_inc(mt_r, 1)
            pool.memset(basei[:, 5:6], 0.0).then_inc(sc_r, 2)

            def rstd(b, mv, ve, rs, ready, l, done):
                hold(pool, ready, b + 1)
                hold(pool, done, b)
                pool.tensor_scalar(ve[:, :], mv[:, :, 1], EPS, None, ALU.add).then_inc(l, 1)
                hold(pool, l, b + 1)
                pool.tensor_tensor(rs[:, :], ve[:, :], c("half"), ALU.pow).then_inc(done, 1)

            def group_norm(i):
                link = linker(pool, gn_l, i, 6, hold)
                hold(pool, g_cp, i + 1)
                link(pool.tensor_tensor(gnt[:, 0, :], gst[:, 0, :], gst[:, 0, :], ALU.mult))
                link(pool.tensor_tensor(gnt[:, 1, :], gst[:, 1, :], gnt[:, 0, :], ALU.subtract))
                link(pool.tensor_scalar(gnt[:, 2, :], gnt[:, 1, :], EPS, None, ALU.add))
                link(pool.tensor_tensor(gnt[:, 3, :], gnt[:, 2, :], c("half")[:, 0:KH], ALU.pow))
                link(pool.tensor_tensor(gns[:, 0, :], gnt[:, 3, :], gnw, ALU.mult))
                link(pool.tensor_tensor(gnt[:, 4, :], gst[:, 0, :], gns[:, 0, :], ALU.mult))
                pool.tensor_tensor(gns[:, 1, :], gnb, gnt[:, 4, :], ALU.subtract).then_inc(gn_r, 1)

            def split_weights(dst, chunk, n):
                src = raw[:, bass.ds(chunk * WC, WC)]
                h = whi[dst][:, bass.ds(chunk * WC, WC)]
                pool.tensor_copy(h, src).then_inc(wp_h, 1)
                hold(pool, wp_h, n)
                return pool.tensor_tensor(wlo[dst][:, bass.ds(chunk * WC, WC)], src, h.bitcast(F32), ALU.subtract)

            def scatter(b, q):
                hold(pool, sl_r, b + 1)
                for k in range(2):
                    for j in range(NJ):
                        pool.indirect_dma_start(xg, bass.IndirectOffsetOnAxis(ap=slot[q][:, k * NJ + j:k * NJ + j + 1], axis=0),
                                                h2[q][:, j, :], None).then_inc(scat, 16)
                hold(pool, scat, (b + 1) * 128)
                pool.sem_inc(sc_r, 1)

            def step(i, q):
                cur, prv, nx2 = has(i), has(i - 1), has(i + 2)
                if prv:
                    rstd(i - 1, mv2, ve2, rs2, bn2, r2l, r2)
                if cur:
                    group_norm(i)
                if nx2:
                    rstd(i + 2, mv1, ve1, rs1, bn1, r1l, r1)
                if cur:
                    hold(pool, mb_ld, i * 16 + 16)
                    pool.tensor_tensor(owg[:, :, :], ow, modb[q][:, 0:1, :].broadcast_to([P, KH, D]), ALU.mult)\
                        .then_inc(owg_r, 1)
                if prv:
                    hold(pool, xn2_r, i)
                    h = h2[1 - q][:, :, 0:D]
                    pool.tensor_tensor(h, h, modb[1 - q][:, 2:3, :].broadcast_to([P, NJ, D]), ALU.mult).then_inc(md_l, 1)
                    hold(pool, md_l, i)
                    pool.tensor_tensor(h, h, modb[1 - q][:, 3:4, :].broadcast_to([P, NJ, D]), ALU.add).then_inc(h2_r, 1)
                if has(i - 2):
                    scatter(i - 2, q)

            pool.wait_ge(c_ld, 16)
            rstd(0, mv1, ve1, rs1, bn1, r1l, r1)
            pool.wait_ge(a_ld, 16)
            for i in range(-1, 1):
                step(i, i % 2)
            pool.wait_ge(raw_ld, 16)
            for n in range(NCH):
                ins = split_weights(0, n, n + 1)
            ins.then_inc(w_r[0], 1)
            steps(pool, step, 1, B, 2, B - 3)
            scatter(B - 1, 1)

            pool.wait_ge(tab_r, 1)
            pool.wait_ge(pad_r, 1)
            for n in range(E * NT):
                pool.indirect_dma_start(xg, bass.IndirectOffsetOnAxis(ap=padi[:, n:n + 1], axis=0), padt[:, :], None)\
                    .then_inc(pad_st, 16)
            pool.wait_ge(x1_st, 16 * B)

            def fetch(g):
                hold(pool, row_ld, g * 16 + 16)
                pool.tensor_copy(meta[:, :, :], rows[:, :, D:RW]).then_inc(mt_r, 1)
                hold(pool, mt_r, g + 2)
                for t in range(NT):
                    pool.indirect_dma_start(gbr[:, t, :], None, gbscr,
                                            bass.IndirectOffsetOnAxis(ap=meta[:, t, E + 1:E + 2].bitcast(I32), axis=0))\
                        .then_inc(gb_ld, 16)

            fetch(0)

            def expert(e, half, more):
                n = pool.value_load(tab[0:1, bass.ds(e, 1)], min_val=1, max_val=B * S // BLK)
                g0 = pool.value_load(tab[0:1, bass.ds(e + E, 1)], min_val=0, max_val=2 * B * S)
                if more:
                    hold(pool, y_ps, g0 + 1)
                    hold(pool, raw_ld, e * 16 + 32)
                    for m in range(NCH):
                        ins = split_weights(1 - half, m, (e + 1) * NCH + m + 1)
                    ins.then_inc(w_r[1 - half], 1)
                with pool.Fori(0, n) as k:
                    g = g0 + k
                    hold(pool, y_r, g + 2)
                    for t in range(NT):
                        pool.indirect_dma_start(out, bass.IndirectOffsetOnAxis(ap=meta[:, t, E:E + 1].bitcast(I32), axis=0),
                                                ysb[:, t, :], None, bounds_check=B * S - 1, oob_is_err=False,
                                                compute_op=ALU.add).then_inc(add_st, 16)
                    hold(pool, add_st, g * 32 + 32)
                    fetch(g + 1)

            experts(pool, expert)


_ORDER = ["x", "modp", "attp", "cst", "we"]


def _halves(a):
    return a.reshape(KH, P, -1).transpose(1, 0, 2).reshape(P, -1)


def kernel(L0_attn_x, L0_attn_Wqkv_w, L0_attn_Wqkv_b, L0_attn_gn_w, L0_attn_gn_b, L0_attn_out_w, L0_attn_out_b,
           L0_ffn_gate_w, L0_ffn_w1, L0_ffn_w2, L0_ffn_w3, L0_c, L0_wmod):
    import concourse.bacc as bacc
    from concourse.bass_utils import run_bass_kernel_spmd as run

    a = {k: np.asarray(v) for k, v in locals().items() if k.startswith("L0")}

    def rows_of(v):
        return np.broadcast_to(v, (P, v.shape[0]))

    wqkv_b = a["L0_attn_Wqkv_b"]
    modp = {"cT": _halves(a["L0_c"].T), "ob": rows_of(a["L0_attn_out_b"]), "wmod": _halves(a["L0_wmod"])}
    attp = {
        "wqkv": _halves(a["L0_attn_Wqkv_w"].T), "bkv": rows_of(wqkv_b[D:]), "ow": _halves(a["L0_attn_out_w"].T),
        "gate": _halves(a["L0_ffn_gate_w"].T), "bq": _halves(wqkv_b[:D, None]),
        "gnw": _halves(a["L0_attn_gn_w"][:, None]), "gnb": _halves(a["L0_attn_gn_b"][:, None]),
    }
    up = [a[n].transpose(0, 2, 1).reshape(E, KH, P, F) for n in ("L0_ffn_w1", "L0_ffn_w3")]
    down = a["L0_ffn_w2"].transpose(0, 2, 1).reshape(E, 2, NF // 2, P, D).transpose(0, 1, 3, 2, 4).reshape(E, 2, P, WC)
    arrays = {
        "x": a["L0_attn_x"].reshape(B * S, D),
        "modp": np.concatenate([modp[n] for n in MODP], 1),
        "attp": np.concatenate([attp[n] for n in ATTP], 1),
        "cst": constants()[0],
        "we": np.concatenate(up + [down], 1),
    }
    arrays = {k: np.ascontiguousarray(v) for k, v in arrays.items()}
    nc = bacc.Bacc("TRN2", target_bir_lowering=False, num_devices=1)
    args = [nc.dram_tensor(k, arrays[k].shape, F32, kind="ExternalInput").ap() for k in _ORDER]
    out = nc.dram_tensor("out", (B * S, D), F32, kind="ExternalOutput").ap()
    adaln_moe_kernel(nc, *args, out)
    r = run(nc, [arrays], core_ids=[0])
    return r.results[0]["out"].reshape(B, S, D)
```

```python
from contextlib import ExitStack

import numpy as np

import concourse.bass as bass
from concourse import mybir
from concourse.alu_op_type import AluOpType as ALU

F32 = mybir.dt.float32
F32R = mybir.dt.float32r
BF16 = mybir.dt.bfloat16
I32 = mybir.dt.int32
U32 = mybir.dt.uint32
ACT = mybir.ActivationFunctionType
AX_X = mybir.AxisListType.X

P = 128
B, S, D = 8, 512, 256
E, F = 8, 1024
HEAD = 8
KH = D // P
NJ = S // P
BLK = 256
NT = BLK // P
NF = F // P
CAP = B * S + BLK
META = D
TOK, BAT = D + E, D + E + 1
RW = D + E + 2
NOROW = 1 << 20
WC = 1024
NCH = 3 * KH * F // WC
EPS = 1e-5
JITTER = 2.0 * 0.01


def constants():
    p = np.arange(P)
    parts = {
        "ident": np.eye(P),
        "mask": np.tile(p[:, None] // HEAD == p[None, :] // HEAD, (1, KH)),
        "avg": (p[:, None] // HEAD == p[None, :] // HEAD) / HEAD,
        "before": p[:, None] < p[None, :],
        "ones": np.ones((P, P)),
        "iota": np.tile(np.arange(E), (P, NJ)),
        "region": np.tile(np.arange(E) * CAP, (P, 1)),
        "padrow": p[:, None] + P * np.tile(np.arange(NT), E)[None, :],
        "token": np.stack([p[:, None] * NJ + np.arange(NJ)[None, :], np.zeros((P, NJ))], 2).reshape(P, 2 * NJ),
        "step": np.tile([S, 1], (P, NJ)),
        "half": np.full((P, NJ), -0.5),
    }
    at, where = 0, {}
    for name, a in parts.items():
        where[name] = (at, a.shape[1])
        at += a.shape[1]
    return np.concatenate([a.astype(np.float32) for a in parts.values()], 1), where


MODP = {"cT": KH * B, "ob": D, "wmod": KH * 6 * D}
ATTP = {"wqkv": KH * 3 * D, "bkv": 2 * D, "ow": KH * D, "gate": KH * E, "bq": KH, "gnw": KH, "gnb": KH}


def wait(eng, sem, value):
    if not (isinstance(value, int) and value <= 0):
        eng.wait_ge(sem, value)


def steps(eng, step, first, last, lo, hi):
    for i in range(first, lo):
        step(i, i % 2)
    with eng.Fori(0, (hi - lo + 1) // 2) as m:
        for s in range(2):
            step(m * 2 + (lo + s), (lo + s) % 2)
    for i in range(hi + 1, last + 1):
        step(i, i % 2)


def has(b):
    return not isinstance(b, int) or 0 <= b < B


def experts(eng, expert):
    with eng.Fori(0, E // 2 - 1) as m:
        for half in range(2):
            expert(m * 2 + half, half, True)
    for half in range(2):
        expert(E - 2 + half, half, half == 0)


def adaln_moe_kernel(nc, x, modp, attp, cst, we, out):
    _, CW = constants()
    ctx = ExitStack()
    with ctx:
        def sb(name, shape, dt=F32, stack=ctx):
            return stack.enter_context(nc.sbuf_tensor(name, shape, dt))

        def sem(name):
            return ctx.enter_context(nc.semaphore(name))

        modscr = nc.dram_tensor("modscr", [B, 4 * D], F32, kind="Internal").ap()
        gbscr = nc.dram_tensor("gbscr", [B, D], F32, kind="Internal").ap()
        xg = nc.dram_tensor("xg", [E * CAP, RW], F32, kind="Internal").ap()

        C = sb("C", [P, sum(n for _, n in CW.values())])
        whi = [sb("whi0", [P, NCH * WC], F32R), None]
        wlo = [sb("wlo0", [P, NCH * WC], F32R), None]
        raw = sb("raw", [P, NCH * WC])
        base = sb("base", [P, E])
        basei = sb("basei", [P, E])
        tabf = sb("tabf", [P, 4, E])
        tabi = sb("tabi", [P, E], I32)
        tab = sb("tab", [P, 2 * E], I32)
        padi = sb("padi", [P, E * NT], I32)
        padt = sb("padt", [P, RW])

        def c(name):
            a, n = CW[name]
            return C[:, a:a + n]

        att = ExitStack()
        X = sb("X", [P, B * NJ * D], stack=att)
        M1 = sb("M1", [P, sum(MODP.values())], stack=att)
        A1 = sb("A1", [P, sum(ATTP.values())], stack=att)
        sT = sb("sT", [P, KH, B], stack=att)
        sT1 = sb("sT1", [P, KH, B], stack=att)
        sT2 = sb("sT2", [P, KH, B], stack=att)
        modc = sb("modc", [P, 2, KH, B], stack=att)
        modr = sb("modr", [B, 5, D], stack=att)
        modt = sb("modt", [B, 2, 2, D], stack=att)
        modb = [sb(f"modb{q}", [P, 4, D], stack=att) for q in range(2)]
        xn = sb("xn", [P, NJ, D], stack=att)
        hT = sb("hT", [P, KH, S], stack=att)
        qT = sb("qT", [P, KH, S], stack=att)
        kv = sb("kv", [P, NJ, 2 * D], stack=att)
        bd = sb("bd", [P, KH, P], stack=att)
        gT = sb("gT", [P, KH, S], stack=att)
        owg = sb("owg", [P, KH, D], stack=att)
        h2 = [sb(f"h2{q}", [P, NJ, RW], stack=att) for q in range(2)]
        h2T = sb("h2T", [P, KH, S], stack=att)
        st1 = sb("st1", [P, NJ, 6], stack=att)
        mv1 = sb("mv1", [P, NJ, 2], stack=att)
        ve1 = sb("ve1", [P, NJ], stack=att)
        rs1 = sb("rs1", [P, NJ], stack=att)
        st2 = sb("st2", [P, NJ, 6], stack=att)
        mv2 = sb("mv2", [P, NJ, 2], stack=att)
        ve2 = sb("ve2", [P, NJ], stack=att)
        rs2 = sb("rs2", [P, NJ], stack=att)
        stc = sb("stc", [P, KH, 6], stack=att)
        mvc = sb("mvc", [P, KH, 2], stack=att)
        msq = sb("msq", [P, KH], stack=att)
        chst = sb("chst", [P, 2, KH], stack=att)
        gst = sb("gst", [P, 2, KH], stack=att)
        gnt = sb("gnt", [P, 6, KH], stack=att)
        gns = sb("gns", [P, 2, KH], stack=att)
        nm1 = sb("nm1", [P, 2, NJ], stack=att)
        nm2 = sb("nm2", [P, 2, NJ], stack=att)
        lgT = sb("lgT", [E, S], stack=att)
        lg = sb("lg", [P, NJ, E], stack=att)
        alg = sb("alg", [P, NJ, E], stack=att)
        mx = sb("mx", [P, NJ, 8], stack=att)
        ix = sb("ix", [P, NJ, 8], U32, stack=att)
        ixf = sb("ixf", [P, 2, NJ], stack=att)
        dl = sb("dl", [P, 2, NJ, E], stack=att)
        fc = sb("fc", [P, 2, NJ, E], stack=att)
        un = sb("un", [P, 2, NJ, E], stack=att)
        dc = sb("dc", [P, 2, NJ, E], stack=att)
        ex = sb("ex", [P, 2, NJ, E], stack=att)
        eu = sb("eu", [P, 2, NJ, E], stack=att)
        oh = sb("oh", [P, 2, NJ, E], stack=att)
        sm = sb("sm", [P, 2 * NJ], stack=att)
        wk = sb("wk", [P, 2 * NJ], stack=att)
        wt = sb("wt", [P, 2, NJ, E], stack=att)
        mk = sb("mk", [P, NJ * E], BF16, stack=att)
        trib = sb("trib", [P, 2 * P], BF16, stack=att)
        tokf = sb("tokf", [P, 2 * NJ], stack=att)
        slf = sb("slf", [P, NJ, E], stack=att)
        ssel = sb("ssel", [P, 2, NJ, E], stack=att)
        srow = sb("srow", [P, 2 * NJ], stack=att)
        slot = [sb(f"slot{q}", [P, 2 * NJ], I32, stack=att) for q in range(2)]
        att.close()

        whi[1] = sb("whi1", [P, NCH * WC], F32R)
        wlo[1] = sb("wlo1", [P, NCH * WC], F32R)
        rows = sb("rows", [P, NT, RW])
        meta = sb("meta", [P, NT, RW - D])
        xhi = sb("xhi", [P, KH, BLK], F32R)
        xlo = sb("xlo", [P, KH, BLK], F32R)
        sg = sb("sg", [P, 2, BLK])
        hf = sb("hf", [P, NF, BLK])
        hhi = sb("hhi", [P, NF, BLK], F32R)
        hlo = sb("hlo", [P, NF, BLK], F32R)
        gbr = sb("gbr", [P, NT, D])
        ysb = sb("ysb", [P, NT, D])

        ps = [ctx.enter_context(nc.psum_tensor(f"ps{i}", [P, 512], F32)) for i in range(8)]

        c_ld, m_ld, a_ld = sem("c_ld"), sem("m_ld"), sem("a_ld")
        x_ld = [sem(f"x_ld{n}") for n in range(4)]
        raw_ld = sem("raw_ld")
        mc_exp, mc_sil, mc_ps, mc_v, mc_st, mb_ld = (sem(n) for n in ("mc_exp", "mc_sil", "mc_ps", "mc_v", "mc_st", "mb_ld"))
        ini, held = sem("ini"), sem("held")
        ln1_l, bn1, r1l, r1, xn_r = (sem(n) for n in ("ln1_l", "bn1", "r1l", "r1", "xn_r"))
        t1_ps, hT_r, q_ps, qT_r, kv_ps, kv_r, ktv_ps, bd_r = (
            sem(n) for n in ("t1_ps", "hT_r", "q_ps", "qT_r", "kv_ps", "kv_r", "ktv_ps", "bd_r"))
        c_ps, cs_l, cs_r, g_ps, g_cp, gn_l, gn_r, gT_r, owg_r = (
            sem(n) for n in ("c_ps", "cs_l", "cs_r", "g_ps", "g_cp", "gn_l", "gn_r", "gT_r", "owg_r"))
        gaob, o_ps, x1_r, x1_st = (sem(n) for n in ("gaob", "o_ps", "x1_r", "x1_st"))
        ln2_l, bn2, r2l, r2, xn2_r, md_l, h2_r = (sem(n) for n in ("ln2_l", "bn2", "r2l", "r2", "xn2_r", "md_l", "h2_r"))
        t2_ps, h2T_r, lT_ps, lT_r, l_ps, lg_r, ro_l, dc_r, ex_r, mk_r, r_ps, rp_l, sl_r, scat, sc_r = (
            sem(n) for n in ("t2_ps", "h2T_r", "lT_ps", "lT_r", "l_ps", "lg_r", "ro_l", "dc_r", "ex_r", "mk_r", "r_ps", "rp_l", "sl_r", "scat", "sc_r"))
        wp_h, wp_l, w_r0, w_r1 = sem("wp_h"), sem("wp_l"), sem("w_r0"), sem("w_r1")
        w_r = [w_r0, w_r1]
        tb_l, tab_r, pad_r, pad_0, pad_st = (sem(n) for n in ("tb_l", "tab_r", "pad_r", "pad_0", "pad_st"))
        row_ld, tp_ps, xh_r, xT_r, gu_ps, sg_r, hf_r, hi_r, hs_r = (
            sem(n) for n in ("row_ld", "tp_ps", "xh_r", "xT_r", "gu_ps", "sg_r", "hf_r", "hi_r", "hs_r"))
        y_ps, y_r, gb_ld, add_st, mt_r = (sem(n) for n in ("y_ps", "y_r", "gb_ld", "add_st", "mt_r"))

        def part(tile, table, name):
            at = 0
            for n, w in table.items():
                if n == name:
                    return tile[:, at:at + w]
                at += w
            raise KeyError(name)

        cT = part(M1, MODP, "cT").rearrange("p (k b) -> p k b", k=KH)
        ob = part(M1, MODP, "ob")
        wmod = part(M1, MODP, "wmod").rearrange("p (k n) -> p k n", k=KH)
        wqkv = part(A1, ATTP, "wqkv").rearrange("p (k n) -> p k n", k=KH)
        bkv = part(A1, ATTP, "bkv")
        ow = part(A1, ATTP, "ow").rearrange("p (k n) -> p k n", k=KH)
        gate = part(A1, ATTP, "gate").rearrange("p (k n) -> p k n", k=KH)
        bq, gnw, gnb = (part(A1, ATTP, n) for n in ("bq", "gnw", "gnb"))
        ident = c("ident")

        def xb(b, off=0, n=NJ * D):
            return X[:, bass.ds(b * (NJ * D) + off, n)]

        def split(ap, **kw):
            return ap.rearrange("p (a b) -> p a b", **kw)

        def flat(tile):
            return tile[:, :, :, :].rearrange("p a b c -> p (a b c)")

        def hold(eng, s, value):
            if not (isinstance(value, int) and value <= 0):
                eng.wait_ge(s, value)
                eng.sem_inc(held, 1)

        def linker(eng, s, b, per, wait_ge=lambda eng, s, v: eng.wait_ge(s, v)):
            n = [0]

            def link(ins):
                n[0] += 1
                assert n[0] <= per
                ins.then_inc(s, 1)
                wait_ge(eng, s, b * per + n[0])
            return link

        block = ctx.enter_context(nc.Block())

        @block.sync
        def _(sp):
            xv = x.rearrange("(b p j) d -> p b (j d)", p=P, j=NJ)
            Xv = X[:, :].rearrange("p (b n) -> p b n", b=B)
            ov = out.rearrange("(b p j) d -> b p (j d)", p=P, j=NJ)
            sp.dma_start(M1[:, :], modp).then_inc(m_ld, 16)
            sp.dma_start(Xv[:, 0:1, :], xv[:, 0:1, :]).then_inc(x_ld[0], 16)
            sp.dma_start(C[:, :], cst).then_inc(c_ld, 16)
            for n, (lo, hi) in ((1, (1, 2)), (2, (2, 3)), (3, (3, B))):
                sp.dma_start(Xv[:, lo:hi, :], xv[:, lo:hi, :]).then_inc(x_ld[n], 16)
            sp.wait_ge(mc_v, 12)
            sp.dma_start(modscr, modr[:, 0:4, :]).then_inc(mc_st, 16)
            sp.dma_start(gbscr, modr[:, 4, :]).then_inc(mc_st, 16)
            sp.wait_ge(mc_st, 32)

            def load_mod(b, q):
                sp.dma_start(modb[q][:, :, :].rearrange("p a n -> p (a n)"),
                             modscr[bass.ds(b, 1), :].broadcast_to([P, 4 * D])).then_inc(mb_ld, 16)

            load_mod(0, 0)
            sp.wait_ge(mb_ld, 16)
            load_mod(1, 1)

            def store(b, q):
                hold(sp, x1_r, b * 2 + 2)
                sp.dma_start(ov[bass.ds(b, 1), :, :].rearrange("o p n -> (o p) n"), xb(b)).then_inc(x1_st, 16)

            def step(b, q):
                hold(sp, mb_ld, b * 16 + 32)
                hold(sp, h2_r, b + 1)
                load_mod(b + 2, q)
                store(b, q)

            steps(sp, step, 0, B - 3, 0, B - 3)

            def load_weights(e):
                sp.dma_start(raw[:, :].rearrange("p (c n) -> p c n", c=NCH),
                             we[bass.ds(e, 1)].rearrange("o c p n -> p (o c) n")).then_inc(raw_ld, 16)

            store(B - 2, 0)
            sp.wait_ge(wp_l, NCH)
            load_weights(1)
            store(B - 1, 1)

            sp.wait_ge(scat, 128 * B)
            sp.wait_ge(pad_0, 16 * NT)
            sp.wait_ge(tab_r, 1)

            def load_rows(first, g):
                hold(sp, tp_ps, g + 1)
                hold(sp, mt_r, g + 1)
                sp.dma_start(rows[:, :, :], xg[bass.ds(first, BLK), :].rearrange("(p t) d -> p t d", t=NT))\
                  .then_inc(row_ld, 16)

            def expert(e, half, more):
                n = sp.value_load(tab[0:1, bass.ds(e, 1)], min_val=1, max_val=B * S // BLK)
                g0 = sp.value_load(tab[0:1, bass.ds(e + E, 1)], min_val=0, max_val=2 * B * S)
                with sp.Fori(0, n) as k:
                    load_rows(e * CAP + k * BLK, g0 + k)
                if half == 0:
                    sp.wait_ge(pad_st, 16 * NT * (E - 1))
                if not isinstance(e, int):
                    hold(sp, w_r[1 - half], (e - half) // 2 + 1 + half)
                    load_weights(e + 2)

            experts(sp, expert)
            n = sp.value_load(tab[0:1, E - 1:E], min_val=1, max_val=B * S // BLK)
            g0 = sp.value_load(tab[0:1, 2 * E - 1:2 * E], min_val=0, max_val=2 * B * S)
            load_rows(0, g0 + n)
            hold(sp, row_ld, (g0 + n) * 16 + 16)
            sp.wait_ge(x1_st, 16 * B)
            hold(sp, add_st, (g0 + n) * 32)
            hold(sp, gb_ld, (g0 + n) * 32 + 32)

        @block.tensor
        def _(pe):
            pe.wait_ge(m_ld, 16)
            pe.wait_ge(mc_sil, 3)
            for n, ch in enumerate((1, 0)):
                for h in range(KH):
                    for k in range(KH):
                        pe.matmul(ps[6][:, (n * KH + h) * B:(n * KH + h + 1) * B],
                                  wmod[:, k, ch * D + h * P:ch * D + (h + 1) * P], sT[:, k, :],
                                  start=(k == 0), stop=(k == KH - 1))
            for n, ch in enumerate((2, 4, 3, 5)):
                for k in range(KH):
                    mm = pe.matmul(ps[2 + n // 2][0:B, n % 2 * D:(n % 2 + 1) * D], sT[:, k, :],
                                   wmod[:, k, ch * D:(ch + 1) * D], start=(k == 0), stop=(k == KH - 1))
            mm.then_inc(mc_ps, 1)
            pe.wait_ge(c_ld, 16)
            pe.wait_ge(a_ld, 16)
            pe.wait_ge(ini, 2)

            def step(i, q):
                cur, nxt, prv, old = has(i), has(i + 1), has(i - 1), has(i - 2)
                if nxt:
                    pe.wait_ge(xn_r, i + 2)
                    for h in range(KH):
                        for j in range(NJ):
                            mm = pe.transpose(ps[h][:, j * P:(j + 1) * P], xn[:, j, h * P:(h + 1) * P], ident)
                        mm.then_inc(t1_ps, 1)
                if cur:
                    pe.wait_ge(bd_r, i + 1)
                if old:
                    hold(pe, lT_r, i - 1)
                    for j in range(NJ):
                        mm = pe.transpose(ps[6][:, 256 + j * E:256 + (j + 1) * E], lgT[:, j * P:(j + 1) * P],
                                          C[0:E, CW["ident"][0]:CW["ident"][0] + E])
                    mm.then_inc(l_ps, 1)
                if cur:
                    pe.wait_ge(qT_r, i * 2 + 2)
                    wait(pe, x1_r, i * 2)
                    for h in range(KH):
                        pe.matmul(ps[2 + h][:, :], bd[:, h, :], qT[:, h, :], start=True, stop=True).then_inc(c_ps, 1)
                if nxt:
                    for m in range(KH):
                        for k in range(KH):
                            pe.wait_ge(hT_r, (i + 1) * 2 + k + 1)
                            mm = pe.matmul(ps[4 + m][:, :], wqkv[:, k, m * P:(m + 1) * P], hT[:, k, :],
                                           start=(k == 0), stop=(k == KH - 1))
                        mm.then_inc(q_ps, 1)
                if old:
                    pe.wait_ge(mk_r, i - 1)
                    for j in range(NJ + 1):
                        o = ps[7][:, 64 + j * E:64 + (j + 1) * E]
                        for n in range(min(j + 1, NJ)):
                            mm = pe.matmul(o, trib[:, P:2 * P] if n < j else trib[:, 0:P], mk[:, n * E:(n + 1) * E],
                                           start=(n == 0), stop=(n == min(j, NJ - 1)))
                    mm.then_inc(r_ps, 1)
                if cur:
                    pe.wait_ge(cs_r, i + 1)
                    pe.matmul(ps[6][:, 0:2 * KH], c("avg"), chst[:, :, :].rearrange("p a b -> p (a b)"),
                              start=True, stop=True).then_inc(g_ps, 1)
                if nxt:
                    for j in range(NJ):
                        if j < 2:
                            pe.wait_ge(qT_r, (i + 1) * 2 + j + 1)
                        for k in range(KH):
                            mm = pe.matmul(ps[(4, 5, 0, 1)[j]][:, :], hT[:, k, j * P:(j + 1) * P],
                                           wqkv[:, k, D:3 * D], start=(k == 0), stop=(k == KH - 1))
                        mm.then_inc(kv_ps, 1)
                    wait(pe, g_cp, i + 1)
                    for h in range(KH):
                        for j in range(NJ):
                            if h == 0:
                                pe.wait_ge(kv_r, (i + 1) * NJ + j + 1)
                            mm = pe.matmul(ps[6][:, h * P:(h + 1) * P], kv[:, j, h * P:(h + 1) * P],
                                           kv[:, j, D + h * P:D + (h + 1) * P], start=(j == 0), stop=(j == NJ - 1))
                    mm.then_inc(ktv_ps, 1)
                if cur:
                    pe.wait_ge(gT_r, i * 2 + 2)
                    pe.wait_ge(owg_r, i + 1)
                    for j in range(NJ):
                        for k in range(KH):
                            mm = pe.matmul(ps[2 + j // 2][:, j % 2 * D:(j % 2 + 1) * D], gT[:, k, j * P:(j + 1) * P],
                                           owg[:, k, :], start=(k == 0), stop=(k == KH - 1))
                        if j % 2:
                            mm.then_inc(o_ps, 1)
                if prv:
                    pe.wait_ge(h2_r, i)
                    for h in range(KH):
                        for j in range(NJ):
                            mm = pe.transpose(ps[h][:, j * P:(j + 1) * P], h2[1 - q][:, j, h * P:(h + 1) * P], ident)
                        mm.then_inc(t2_ps, 1)
                    wait(pe, sl_r, i - 1)
                    for k in range(KH):
                        pe.wait_ge(h2T_r, (i - 1) * 2 + k + 1)
                        mm = pe.matmul(ps[7][0:E, :], gate[:, k, :], h2T[:, k, :], start=(k == 0), stop=(k == KH - 1))
                    mm.then_inc(lT_ps, 1)

            steps(pe, step, -1, B + 1, 2, B - 3)

            def turn(g):
                pe.wait_ge(row_ld, g * 16 + 16)
                for k in range(KH):
                    for t in range(NT):
                        mm = pe.transpose(ps[7][:, k * BLK + t * P:k * BLK + (t + 1) * P], rows[:, t, k * P:(k + 1) * P],
                                          ident)
                mm.then_inc(tp_ps, 1)

            def expert(e, half, more):
                hi, lo = whi[half], wlo[half]
                n = pe.value_load(tab[0:1, bass.ds(e, 1)], min_val=1, max_val=B * S // BLK)
                g0 = pe.value_load(tab[0:1, bass.ds(e + E, 1)], min_val=0, max_val=2 * B * S)
                hold(pe, w_r[half], (e - half) // 2 + 1)

                def up(g, f):
                    pe.wait_ge(hf_r, g * NF + f + 1)
                    for n_, o in enumerate((0, BLK)):
                        for k in range(KH):
                            at = (n_ * KH + k) * F + f * P
                            for a, b_ in ((hi, xhi), (lo, xhi), (hi, xlo)):
                                mm = pe.matmul(ps[f % 4][:, o:o + BLK], a[:, at:at + P], b_[:, k, :],
                                               start=(k == 0 and a is hi and b_ is xhi),
                                               stop=(k == KH - 1 and b_ is xlo))
                    mm.then_inc(gu_ps, 1)

                def down(g, f):
                    pe.wait_ge(hs_r, g * NF + f + 1)
                    if f == 0:
                        pe.wait_ge(y_r, g + 1)
                    at = (2 * KH * F) + f * D
                    for t in range(NT):
                        for a, b_ in ((hhi, hi), (hlo, hi), (hhi, lo)):
                            mm = pe.matmul(ps[4 + t][:, 0:D], a[:, f, t * P:(t + 1) * P], b_[:, at:at + D],
                                           start=(f == 0 and a is hhi and b_ is hi),
                                           stop=(f == NF - 1 and b_ is lo))
                    if f == NF - 1:
                        mm.then_inc(y_ps, 1)

                with pe.Fori(0, n) as k_:
                    g = g0 + k_
                    pe.wait_ge(xT_r, g + 1)
                    for f in range(NF):
                        up(g, f)
                        if f == NF - 1:
                            turn(g + 1)
                        if f >= 2:
                            down(g, f - 2)
                    down(g, NF - 2)
                    down(g, NF - 1)

            pe.wait_ge(sl_r, B)
            pe.wait_ge(tab_r, 1)
            turn(0)
            experts(pe, expert)

        @block.scalar
        def _(act):
            act.wait_ge(m_ld, 16)
            act.activation(sT1[:, :, :], cT, ACT.Exp, scale=-1.0).then_inc(mc_exp, 1)
            act.dma_start(A1[:, :], attp).then_inc(a_ld, 16)
            act.dma_start(raw[:, :].rearrange("p (c n) -> p c n", c=NCH),
                          we[0].rearrange("c p n -> p c n")).then_inc(raw_ld, 16)

            def norm(b, src, dst, mv_, nm_, rs_, ready):
                act.wait_ge(ready, b + 1)
                for j in range(NJ):
                    ins = act.activation(dst(j), src(b, j * D, D), ACT.Identity, bias=nm_[:, 1, j:j + 1],
                                         scale=rs_[:, j:j + 1])
                return ins

            def first_norm(b):
                wait(act, t1_ps, b * 2)
                norm(b, xb, lambda j: xn[:, j, :], mv1, nm1, rs1, r1).then_inc(xn_r, 1)

            def high_weights(dst, chunk, n):
                act.activation(whi[dst][:, bass.ds(chunk * WC, WC)], raw[:, bass.ds(chunk * WC, WC)], ACT.Copy)\
                    .then_inc(wp_h, 1)

            first_norm(0)
            act.wait_ge(mc_v, 2)
            act.wait_ge(a_ld, 16)

            def step(i, q):
                cur, nxt, prv, old, nx2 = has(i), has(i + 1), has(i - 1), has(i - 2), has(i + 2)
                if nxt:
                    for h in range(KH):
                        act.wait_ge(t1_ps, (i + 1) * 2 + h + 1)
                        act.activation(hT[:, h, :], ps[h][:, :], ACT.Identity, bias=modc[:, 1, h, bass.ds(i + 1, 1)],
                                       scale=modc[:, 0, h, bass.ds(i + 1, 1)]).then_inc(hT_r, 1)
                if old:
                    act.wait_ge(dc_r, i - 1)
                    act.activation(flat(ex), flat(dc), ACT.Exp, scale=-1.0).then_inc(ex_r, 1)
                if prv:
                    act.wait_ge(sc_r, i)
                    norm(i - 1, xb, lambda j: h2[1 - q][:, j, 0:D], mv2, nm2, rs2, r2).then_inc(xn2_r, 1)
                if nxt:
                    for m in range(KH):
                        act.wait_ge(q_ps, (i + 1) * 2 + m + 1)
                        act.activation(qT[:, m, :], ps[4 + m][:, :], ACT.Identity, bias=bq[:, m:m + 1]).then_inc(qT_r, 1)
                if cur:
                    act.wait_ge(gn_r, i + 1)
                    for h in range(KH):
                        act.activation(gT[:, h, :], ps[2 + h][:, :], ACT.Identity, bias=gns[:, 1, h:h + 1],
                                       scale=gns[:, 0, h:h + 1]).then_inc(gT_r, 1)
                if nx2:
                    first_norm(i + 2)
                if not isinstance(i, int) or 0 <= i < NCH:
                    act.wait_ge(raw_ld, 16)
                    high_weights(0, i, i + 1)
                if prv:
                    for h in range(KH):
                        act.wait_ge(t2_ps, (i - 1) * 2 + h + 1)
                        act.activation(h2T[:, h, :], ps[h][:, :], ACT.Copy).then_inc(h2T_r, 1)
                    act.wait_ge(lT_ps, i)
                    act.activation(lgT[:, :], ps[7][0:E, :], ACT.Copy).then_inc(lT_r, 1)

            steps(act, step, -1, B + 1, 2, B - 3)

            act.wait_ge(sl_r, B)
            act.wait_ge(tab_r, 1)

            def turned(g):
                act.wait_ge(tp_ps, g + 2)
                act.activation(xhi[:, :, :].rearrange("p k n -> p (k n)"), ps[7][:, :], ACT.Copy).then_inc(xh_r, 1)

            turned(0)

            def expert(e, half, more):
                n = act.value_load(tab[0:1, bass.ds(e, 1)], min_val=1, max_val=B * S // BLK)
                g0 = act.value_load(tab[0:1, bass.ds(e + E, 1)], min_val=0, max_val=2 * B * S)

                def high(g, f):
                    act.wait_ge(hf_r, g * NF + f + 1 + 4)
                    act.activation(hhi[:, f, :], hf[:, f, :], ACT.Copy).then_inc(hi_r, 1)

                def block_(g, first):
                    for f in range(NF):
                        act.wait_ge(gu_ps, g * NF + f + 1)
                        act.wait_ge(hf_r, g * NF + f + 3)
                        act.activation(sg[:, f % 2, :], ps[f % 4][:, 0:BLK], ACT.Silu).then_inc(sg_r, 1)
                        if f:
                            high(g, f - 1)
                        if first and more and f < NCH:
                            if f == 0:
                                hold(act, raw_ld, e * 16 + 32)
                            high_weights(1 - half, f, (e + 1) * NCH + f + 1)
                    turned(g + 1)
                    high(g, NF - 1)

                block_(g0, True)
                with act.If(n > 1):
                    with act.Fori(1, n) as k:
                        block_(g0 + k, False)

            experts(act, expert)

        @block.vector
        def _(dve):
            dve.wait_ge(mc_exp, 1)
            dve.tensor_scalar(sT2[:, :, :], sT1[:, :, :], 1.0, None, ALU.add).then_inc(mc_sil, 1)
            dve.wait_ge(mc_sil, 1)
            dve.reciprocal(sT1[:, :, :], sT2[:, :, :]).then_inc(mc_sil, 1)
            dve.wait_ge(mc_sil, 2)
            dve.tensor_tensor(sT[:, :, :], sT1[:, :, :], cT, ALU.mult).then_inc(mc_sil, 1)

            def layer_stats(b, src, stt_, mv, nm, l, read, out_sem):
                for j in range(NJ):
                    ins = dve.bn_stats(stt_[:, j, :], src(b, j * D, D))
                ins.then_inc(l, 1)
                hold(dve, read, b)
                hold(dve, l, b * 2 + 1)
                for j in range(NJ):
                    ins = dve.bn_aggr(mv[:, j, :], stt_[:, j, :])
                ins.then_inc(l, 1)
                hold(dve, l, b * 2 + 2)
                dve.tensor_scalar(nm[:, 0, :], mv[:, :, 0], -1.0, None, ALU.mult).then_inc(out_sem, 1)

            def first_stats(b):
                if isinstance(b, int):
                    dve.wait_ge(x_ld[min(b, 3)], 16)
                layer_stats(b, xb, st1, mv1, nm1, ln1_l, r1, bn1)

            first_stats(0)
            dve.wait_ge(mc_ps, 1)
            dve.tensor_scalar(modc[:, 0, :, :], split(ps[6][:, 0:KH * B], a=KH), 1.0, None, ALU.add).then_inc(mc_v, 1)
            dve.tensor_copy(modc[:, 1, :, :], split(ps[6][:, KH * B:2 * KH * B], a=KH)).then_inc(mc_v, 1)
            g2 = (ps[2][0:B, 0:D], ps[3][0:B, D:2 * D])
            for n in range(2):
                dve.tensor_scalar(modt[:, n, 0, :], g2[n], 0.0, None, ALU.is_ge).then_inc(mc_v, 1)
                dve.tensor_scalar(modt[:, n, 1, :], g2[n], -1.0, None, ALU.mult).then_inc(mc_v, 1)
            dve.wait_ge(mc_v, 6)
            for n in range(2):
                dve.tensor_scalar(modt[:, n, 0, :], modt[:, n, 0, :], 2.0, -1.0, ALU.mult, ALU.add)
                dve.scalar_tensor_tensor(modt[:, n, 1, :], modt[:, n, 1, :], 0.25, g2[n], ALU.max, ALU.max)\
                   .then_inc(mc_v, 1)
            dve.wait_ge(mc_v, 8)
            dve.tensor_tensor(modr[:, 0, :], modt[:, 0, 0, :], modt[:, 0, 1, :], ALU.mult).then_inc(mc_v, 1)
            dve.tensor_tensor(modr[:, 4, :], modt[:, 1, 0, :], modt[:, 1, 1, :], ALU.mult)
            dve.tensor_scalar(modr[:, 2, :], ps[2][0:B, D:2 * D], 1.0, None, ALU.add).then_inc(mc_v, 1)
            dve.tensor_copy(modr[:, 3, :], ps[3][0:B, 0:D]).then_inc(mc_v, 1)
            dve.wait_ge(mc_v, 9)
            dve.tensor_tensor(modr[:, 1, :], modr[:, 0, :], ob[0:B, :], ALU.mult).then_inc(mc_v, 1)
            dve.wait_ge(c_ld, 16)
            dve.tensor_copy(trib[:, :], C[:, CW["before"][0]:CW["before"][0] + 2 * P]).then_inc(ini, 1)
            dve.tensor_copy(base[:, :], c("region")).then_inc(ini, 1)
            dve.tensor_copy(tokf[:, :], c("token")).then_inc(ini, 1)
            dve.wait_ge(ini, 3)
            dve.wait_ge(a_ld, 16)

            def context_stats(i):
                link = linker(dve, cs_l, i, 3, hold)
                for h in range(KH):
                    dve.wait_ge(c_ps, i * 2 + h + 1)
                    ins = dve.bn_stats(stc[:, h, :], ps[2 + h][:, :])
                link(ins)
                for h in range(KH):
                    ins = dve.bn_aggr(mvc[:, h, :], stc[:, h, :])
                link(ins)
                dve.tensor_copy(chst[:, 0, :], mvc[:, :, 0])
                link(dve.tensor_tensor(msq[:, :], mvc[:, :, 0], mvc[:, :, 0], ALU.mult))
                dve.tensor_tensor(chst[:, 1, :], msq[:, :], mvc[:, :, 1], ALU.add).then_inc(cs_r, 1)

            def keep_kv(b, j):
                dve.wait_ge(kv_ps, b * NJ + j + 1)
                dve.tensor_tensor(kv[:, j, :], ps[(4, 5, 0, 1)[j]][:, :], bkv, ALU.add).then_inc(kv_r, 1)

            def routing(b, q):
                link = linker(dve, ro_l, b, 5)
                dve.wait_ge(l_ps, b + 1)
                link(dve.tensor_copy(lg[:, :, :], split(ps[6][:, 256:256 + NJ * E], a=NJ)))
                dve.scalar_tensor_tensor(alg[:, :, :], lg[:, :, :], -1.0, lg[:, :, :], ALU.mult, ALU.max)
                for j in range(NJ):
                    ins = dve.max(mx[:, j, :], lg[:, j, :])
                link(ins)
                for k in range(2):
                    best = mx[:, :, k:k + 1].broadcast_to([P, NJ, E])
                    dve.tensor_tensor(dl[:, k, :, :], best, lg[:, :, :], ALU.subtract)
                    dve.tensor_tensor(fc[:, k, :, :], best, alg[:, :, :], ALU.max)
                for j in range(NJ):
                    ins = dve.max_index(ix[:, j, :], mx[:, j, :], lg[:, j, :])
                link(ins)
                dve.tensor_copy(ixf[:, :, :], ix[:, :, 0:2].rearrange("p j k -> p k j"))
                dve.tensor_scalar(flat(dc), flat(dl), 0.0, None, ALU.max).then_inc(dc_r, 1)
                link(dve.scalar_tensor_tensor(flat(un), flat(fc), JITTER, flat(dl), ALU.mult, ALU.is_ge))
                for k in range(2):
                    ins = dve.tensor_tensor(oh[:, k, :, :], split(c("iota"), a=NJ),
                                            ixf[:, k, :].rearrange("p (j o) -> p j o", o=1).broadcast_to([P, NJ, E]),
                                            ALU.is_equal)
                link(ins)
                dve.scalar_tensor_tensor(un[:, 1, :, :], oh[:, 0, :, :], 0.5, un[:, 1, :, :], ALU.is_lt, ALU.mult)
                dve.tensor_tensor(split(mk[:, :], a=NJ), oh[:, 0, :, :], oh[:, 1, :, :], ALU.add).then_inc(mk_r, 1)

            def routed(b, q):
                link = linker(dve, rp_l, b, 4)
                dve.wait_ge(ex_r, b + 1)
                dve.wait_ge(mk_r, b + 1)
                dve.wait_ge(r_ps, b + 1)
                dve.tensor_tensor(flat(eu), flat(ex), flat(un), ALU.mult)
                link(dve.tensor_tensor(slf[:, :, :], split(ps[7][:, 64:64 + NJ * E], a=NJ),
                                       base[:, :].rearrange("p (o e) -> p o e", o=1).broadcast_to([P, NJ, E]), ALU.add))
                dve.tensor_reduce(sm[:, :], eu[:, :, :, :].rearrange("p a b c -> p (a b) c"), AX_X, ALU.add)
                for k in range(2):
                    dve.tensor_tensor(ssel[:, k, :, :], oh[:, k, :, :], slf[:, :, :], ALU.mult)
                dve.tensor_copy(h2[q][:, :, TOK:TOK + 2].bitcast(I32), split(tokf[:, :], a=NJ))
                link(dve.tensor_tensor(base[:, :], base[:, :], ps[7][:, 64 + NJ * E:64 + (NJ + 1) * E], ALU.add))
                dve.reciprocal(wk[:, :], sm[:, :])
                dve.tensor_tensor(tokf[:, :], tokf[:, :], c("step"), ALU.add)
                link(dve.tensor_reduce(srow[:, :], ssel[:, :, :, :].rearrange("p a b c -> p (a b) c"), AX_X, ALU.add))
                dve.tensor_copy(slot[q][:, :], srow[:, :])
                link(dve.tensor_tensor(wt[:, :, :, :].rearrange("p a b c -> p (a b) c"),
                                       oh[:, :, :, :].rearrange("p a b c -> p (a b) c"),
                                       wk[:, :].rearrange("p (n o) -> p n o", o=1).broadcast_to([P, 2 * NJ, E]), ALU.mult))
                dve.tensor_tensor(h2[q][:, :, META:META + E], wt[:, 0, :, :], wt[:, 1, :, :], ALU.add).then_inc(sl_r, 1)

            def low_weights(dst, chunk, n):
                dve.wait_ge(wp_h, n)
                return dve.tensor_tensor(wlo[dst][:, bass.ds(chunk * WC, WC)], raw[:, bass.ds(chunk * WC, WC)],
                                         whi[dst][:, bass.ds(chunk * WC, WC)].bitcast(F32), ALU.subtract)

            def step(i, q):
                cur, nxt, prv, old, nx2 = has(i), has(i + 1), has(i - 1), has(i - 2), has(i + 2)
                if prv:
                    layer_stats(i - 1, xb, st2, mv2, nm2, ln2_l, r2, bn2)
                if old:
                    routing(i - 2, q)
                if cur:
                    context_stats(i)
                if nx2:
                    first_stats(i + 2)
                if cur:
                    dve.wait_ge(g_ps, i + 1)
                    dve.tensor_copy(gst[:, :, :].rearrange("p a b -> p (a b)"), ps[6][:, 0:2 * KH]).then_inc(g_cp, 1)
                if prv:
                    dve.wait_ge(xn2_r, i)
                    h = h2[1 - q][:, :, 0:D]
                    dve.tensor_tensor(h, h, modb[1 - q][:, 2:3, :].broadcast_to([P, NJ, D]), ALU.mult).then_inc(md_l, 1)
                    dve.wait_ge(md_l, i)
                    dve.tensor_tensor(h, h, modb[1 - q][:, 3:4, :].broadcast_to([P, NJ, D]), ALU.add).then_inc(h2_r, 1)
                if old:
                    routed(i - 2, q)
                if nxt:
                    keep_kv(i + 1, 0)
                if cur:
                    dve.wait_ge(mb_ld, i * 16 + 16)
                    dve.tensor_tensor(split(xb(i), a=NJ), split(xb(i), a=NJ),
                                      modb[q][:, 1:2, :].broadcast_to([P, NJ, D]), ALU.add).then_inc(gaob, 1)
                if nxt:
                    for j in range(1, NJ):
                        keep_kv(i + 1, j)
                    dve.wait_ge(ktv_ps, i + 2)
                    dve.tensor_tensor(bd[:, :, :].rearrange("p a b -> p (a b)"), ps[6][:, 0:KH * P], c("mask"), ALU.mult)\
                       .then_inc(bd_r, 1)
                if not isinstance(i, int) or 0 <= i < NCH:
                    low_weights(0, i, i + 1).then_inc(wp_l, 1)
                if cur:
                    dve.wait_ge(gaob, i + 1)
                    for n in range(2):
                        dve.wait_ge(o_ps, i * 2 + n + 1)
                        dve.tensor_tensor(xb(i, n * 2 * D, 2 * D), ps[2 + n][:, :], xb(i, n * 2 * D, 2 * D), ALU.add)\
                           .then_inc(x1_r, 1)
                    hold(dve, x1_r, i * 2 + 2)

            steps(dve, step, -1, B + 1, 2, B - 3)

            n_tab = [0]

            def tlink(ins):
                n_tab[0] += 1
                ins.then_inc(tb_l, 1)
                dve.wait_ge(tb_l, n_tab[0])

            dve.tensor_tensor(padi[:, :].rearrange("p (e t) -> p e t", t=NT),
                              base[:, :].rearrange("p (e o) -> p e o", o=1).broadcast_to([P, E, NT]),
                              c("padrow").rearrange("p (e t) -> p e t", t=NT), ALU.add)
            dve.wait_ge(wp_l, NCH)
            dve.memset(padt[:, :], 0.0).then_inc(w_r[0], 1)
            tlink(dve.tensor_tensor(tabf[:, 0, :], base[:, :], c("region"), ALU.subtract))
            dve.memset(padt[:, TOK:TOK + 1].bitcast(I32), NOROW).then_inc(pad_r, 1)
            tlink(dve.tensor_scalar(tabf[:, 1, :], tabf[:, 0, :], float(BLK - 1), None, ALU.add))
            tlink(dve.tensor_copy(tabi[:, :], tabf[:, 1, :]))
            tlink(dve.tensor_scalar(tab[:, 0:E], tabi[:, :], BLK.bit_length() - 1, None, ALU.logical_shift_right))
            tlink(dve.tensor_copy(tabf[:, 2, :], tab[:, 0:E]))
            tlink(dve.tensor_scalar(tabf[:, 3, :], tabf[:, 2, :], 1.0, None, ALU.max))
            tlink(dve.tensor_tensor_scan(tabf[:, 0, :], c("ones")[:, 0:E], tabf[:, 3, :], 0.0, ALU.mult, ALU.add))
            tlink(dve.tensor_tensor(tabf[:, 1, :], tabf[:, 0, :], tabf[:, 3, :], ALU.subtract))
            dve.tensor_copy(tab[:, 0:E], tabf[:, 3, :])
            dve.tensor_copy(tab[:, E:2 * E], tabf[:, 1, :]).then_inc(tab_r, 1)
            dve.wait_ge(tab_r, 1)

            def turned(g):
                dve.wait_ge(xh_r, g + 1)
                dve.tensor_tensor(xlo[:, :, :].rearrange("p k n -> p (k n)"), ps[7][:, :],
                                  xhi[:, :, :].rearrange("p k n -> p (k n)").bitcast(F32), ALU.subtract).then_inc(xT_r, 1)

            turned(0)

            def expert(e, half, more):
                n = dve.value_load(tab[0:1, bass.ds(e, 1)], min_val=1, max_val=B * S // BLK)
                g0 = dve.value_load(tab[0:1, bass.ds(e + E, 1)], min_val=0, max_val=2 * B * S)

                def low(g, f):
                    dve.wait_ge(hi_r, g * NF + f + 1)
                    dve.tensor_tensor(hlo[:, f, :], hf[:, f, :], hhi[:, f, :].bitcast(F32), ALU.subtract)\
                       .then_inc(hs_r, 1)

                def block_(g, first):
                    for f in range(NF):
                        dve.wait_ge(sg_r, g * NF + f + 1)
                        dve.tensor_tensor(hf[:, f, :], ps[f % 4][:, BLK:2 * BLK], sg[:, f % 2, :], ALU.mult)\
                           .then_inc(hf_r, 1)
                        if f:
                            low(g, f - 1)
                        if first and more and f < NCH:
                            ins = low_weights(1 - half, f, (e + 1) * NCH + f + 1)
                            if f == NCH - 1:
                                ins.then_inc(w_r[1 - half], 1)
                    turned(g + 1)
                    low(g, NF - 1)
                    dve.wait_ge(gb_ld, g * 32 + 32)
                    dve.wait_ge(y_ps, g + 2)
                    for t in range(NT):
                        ins = dve.scalar_tensor_tensor(ysb[:, t, :], ps[4 + t][:, 0:D], meta[:, t, bass.ds(e, 1)],
                                                       gbr[:, t, :], ALU.mult, ALU.mult)
                    ins.then_inc(y_r, 1)

                block_(g0, True)
                with dve.If(n > 1):
                    with dve.Fori(1, n) as k:
                        block_(g0 + k, False)

            experts(dve, expert)

        @block.gpsimd
        def _(pool):
            pool.memset(basei[:, 0:1], 0.0).then_inc(hf_r, 4)
            pool.memset(basei[:, 1:2], 0.0).then_inc(y_r, 1)
            pool.memset(basei[:, 2:3], 0.0).then_inc(y_ps, 1)
            pool.memset(basei[:, 3:4], 0.0).then_inc(tp_ps, 1)
            pool.memset(basei[:, 4:5], 0.0).then_inc(mt_r, 1)
            pool.memset(basei[:, 5:6], 0.0).then_inc(sc_r, 2)

            def rstd(b, mv, nm, ve, rs, ready, l, done, normed):
                hold(pool, ready, b + 1)
                hold(pool, done, b)
                hold(pool, normed, b)
                pool.tensor_scalar(ve[:, :], mv[:, :, 1], EPS, None, ALU.add).then_inc(l, 1)
                hold(pool, l, b * 2 + 1)
                pool.tensor_tensor(rs[:, :], ve[:, :], c("half"), ALU.pow).then_inc(l, 1)
                hold(pool, l, b * 2 + 2)
                pool.tensor_tensor(nm[:, 1, :], nm[:, 0, :], rs[:, :], ALU.mult).then_inc(done, 1)

            def group_norm(i):
                link = linker(pool, gn_l, i, 6, hold)
                hold(pool, g_cp, i + 1)
                link(pool.tensor_tensor(gnt[:, 0, :], gst[:, 0, :], gst[:, 0, :], ALU.mult))
                link(pool.tensor_tensor(gnt[:, 1, :], gst[:, 1, :], gnt[:, 0, :], ALU.subtract))
                link(pool.tensor_scalar(gnt[:, 2, :], gnt[:, 1, :], EPS, None, ALU.add))
                link(pool.tensor_tensor(gnt[:, 3, :], gnt[:, 2, :], c("half")[:, 0:KH], ALU.pow))
                link(pool.tensor_tensor(gns[:, 0, :], gnt[:, 3, :], gnw, ALU.mult))
                link(pool.tensor_tensor(gnt[:, 4, :], gst[:, 0, :], gns[:, 0, :], ALU.mult))
                pool.tensor_tensor(gns[:, 1, :], gnb, gnt[:, 4, :], ALU.subtract).then_inc(gn_r, 1)

            def scatter(b, q):
                hold(pool, sl_r, b + 1)
                for k in range(2):
                    for j in range(NJ):
                        pool.indirect_dma_start(xg, bass.IndirectOffsetOnAxis(ap=slot[q][:, k * NJ + j:k * NJ + j + 1], axis=0),
                                                h2[q][:, j, :], None).then_inc(scat, 16)
                hold(pool, scat, (b + 1) * 128)
                pool.sem_inc(sc_r, 1)

            def step(i, q):
                cur, prv, old, nx2 = has(i), has(i - 1), has(i - 2), has(i + 2)
                if prv:
                    rstd(i - 1, mv2, nm2, ve2, rs2, bn2, r2l, r2, xn2_r)
                if cur:
                    group_norm(i)
                if nx2:
                    rstd(i + 2, mv1, nm1, ve1, rs1, bn1, r1l, r1, xn_r)
                if cur:
                    hold(pool, mb_ld, i * 16 + 16)
                    pool.tensor_tensor(owg[:, :, :], ow, modb[q][:, 0:1, :].broadcast_to([P, KH, D]), ALU.mult)\
                        .then_inc(owg_r, 1)
                if old:
                    scatter(i - 2, q)

            pool.wait_ge(c_ld, 16)
            rstd(0, mv1, nm1, ve1, rs1, bn1, r1l, r1, xn_r)
            pool.wait_ge(a_ld, 16)
            steps(pool, step, -1, B + 1, 2, B - 3)

            pool.wait_ge(tab_r, 1)
            pool.wait_ge(pad_r, 1)
            def pad(n):
                return pool.indirect_dma_start(xg, bass.IndirectOffsetOnAxis(ap=padi[:, n:n + 1], axis=0), padt[:, :], None)

            for n in range(NT):
                pad(n).then_inc(pad_0, 16)
            pool.wait_ge(x1_st, 16 * B)

            def fetch(g):
                hold(pool, row_ld, g * 16 + 16)
                pool.tensor_copy(meta[:, :, :], rows[:, :, D:RW]).then_inc(mt_r, 1)
                hold(pool, mt_r, g + 2)
                for t in range(NT):
                    pool.indirect_dma_start(gbr[:, t, :], None, gbscr,
                                            bass.IndirectOffsetOnAxis(ap=meta[:, t, E + 1:E + 2].bitcast(I32), axis=0))\
                        .then_inc(gb_ld, 16)

            fetch(0)
            for n in range(NT, NT * E):
                pad(n).then_inc(pad_st, 16)

            def expert(e, half, more):
                n = pool.value_load(tab[0:1, bass.ds(e, 1)], min_val=1, max_val=B * S // BLK)
                g0 = pool.value_load(tab[0:1, bass.ds(e + E, 1)], min_val=0, max_val=2 * B * S)
                with pool.Fori(0, n) as k:
                    g = g0 + k
                    hold(pool, y_r, g + 2)
                    for t in range(NT):
                        pool.indirect_dma_start(out, bass.IndirectOffsetOnAxis(ap=meta[:, t, E:E + 1].bitcast(I32), axis=0),
                                                ysb[:, t, :], None, bounds_check=B * S - 1, oob_is_err=False,
                                                compute_op=ALU.add).then_inc(add_st, 16)
                    hold(pool, add_st, g * 32 + 32)
                    fetch(g + 1)

            experts(pool, expert)


_ORDER = ["x", "modp", "attp", "cst", "we"]


def _halves(a):
    return a.reshape(KH, P, -1).transpose(1, 0, 2).reshape(P, -1)


def kernel(L0_attn_x, L0_attn_Wqkv_w, L0_attn_Wqkv_b, L0_attn_gn_w, L0_attn_gn_b, L0_attn_out_w, L0_attn_out_b,
           L0_ffn_gate_w, L0_ffn_w1, L0_ffn_w2, L0_ffn_w3, L0_c, L0_wmod):
    import concourse.bacc as bacc
    from concourse.bass_utils import run_bass_kernel_spmd as run

    a = {k: np.asarray(v) for k, v in locals().items() if k.startswith("L0")}

    def rows_of(v):
        return np.broadcast_to(v, (P, v.shape[0]))

    wqkv_b = a["L0_attn_Wqkv_b"]
    modp = {"cT": _halves(a["L0_c"].T), "ob": rows_of(a["L0_attn_out_b"]), "wmod": _halves(a["L0_wmod"])}
    attp = {
        "wqkv": _halves(a["L0_attn_Wqkv_w"].T), "bkv": rows_of(wqkv_b[D:]), "ow": _halves(a["L0_attn_out_w"].T),
        "gate": _halves(a["L0_ffn_gate_w"].T), "bq": _halves(wqkv_b[:D, None]),
        "gnw": _halves(a["L0_attn_gn_w"][:, None]), "gnb": _halves(a["L0_attn_gn_b"][:, None]),
    }
    up = [a[n].transpose(0, 2, 1).reshape(E, KH, P, F) for n in ("L0_ffn_w1", "L0_ffn_w3")]
    down = a["L0_ffn_w2"].transpose(0, 2, 1).reshape(E, 2, NF // 2, P, D).transpose(0, 1, 3, 2, 4).reshape(E, 2, P, WC)
    arrays = {
        "x": a["L0_attn_x"].reshape(B * S, D),
        "modp": np.concatenate([modp[n] for n in MODP], 1),
        "attp": np.concatenate([attp[n] for n in ATTP], 1),
        "cst": constants()[0],
        "we": np.concatenate(up + [down], 1),
    }
    arrays = {k: np.ascontiguousarray(v) for k, v in arrays.items()}
    nc = bacc.Bacc("TRN2", target_bir_lowering=False, num_devices=1)
    args = [nc.dram_tensor(k, arrays[k].shape, F32, kind="ExternalInput").ap() for k in _ORDER]
    out = nc.dram_tensor("out", (B * S, D), F32, kind="ExternalOutput").ap()
    adaln_moe_kernel(nc, *args, out)
    r = run(nc, [arrays], core_ids=[0])
    return r.results[0]["out"].reshape(B, S, D)
```

```python
from contextlib import ExitStack

import numpy as np

import concourse.bass as bass
from concourse import mybir
from concourse.alu_op_type import AluOpType as ALU

F32 = mybir.dt.float32
F32R = mybir.dt.float32r
BF16 = mybir.dt.bfloat16
I32 = mybir.dt.int32
U32 = mybir.dt.uint32
ACT = mybir.ActivationFunctionType
AX_X = mybir.AxisListType.X

P = 128
B, S, D = 8, 512, 256
E, F = 8, 1024
HEAD = 8
KH = D // P
NJ = S // P
BLK = 256
NT = BLK // P
NF = F // P
NTF = 512 // P
GAT = 1
SPLIT = 6
RAT = 3
LAG = 3
CAP = B * S + BLK
META = D
TOK, BAT = D + E, D + E + 1
RW = D + E + 2
NOROW = 1 << 20
NCH = F // P
WC = 3 * KH * F // NCH
EPS = 1e-5
JITTER = 2.0 * 0.01


def constants():
    p = np.arange(P)
    parts = {
        "ident": np.eye(P),
        "mask": np.tile(p[:, None] // HEAD == p[None, :] // HEAD, (1, KH)),
        "avg": (p[:, None] // HEAD == p[None, :] // HEAD) / HEAD,
        "before": p[:, None] < p[None, :],
        "ones": np.ones((P, P)),
        "iota": np.tile(np.arange(E), (P, NJ)),
        "region": np.tile(np.arange(E) * CAP, (P, 1)),
        "token": np.stack([p[:, None] * NJ + np.arange(NJ)[None, :], np.zeros((P, NJ))], 2).reshape(P, 2 * NJ),
        "step": np.tile([S, 1], (P, NJ)),
        "half": np.full((P, NJ), -0.5),
    }
    at, where = 0, {}
    for name, a in parts.items():
        where[name] = (at, a.shape[1])
        at += a.shape[1]
    return np.concatenate([a.astype(np.float32) for a in parts.values()], 1), where


MODC = {"cT": KH * B, "wmodc": KH * 2 * D}
MODB = {"ob": D, "wmodb": KH * 4 * D}
ATTP = {"wqkv": KH * 3 * D, "bkv": 2 * D, "ow": KH * D, "gate": KH * E, "bq": KH, "gnw": KH, "gnb": KH}


def wait(eng, sem, value):
    if not (isinstance(value, int) and value <= 0):
        eng.wait_ge(sem, value)


def steps(eng, step, first, last, lo, hi):
    for i in range(first, lo):
        step(i, i % 2)
    with eng.Fori(0, (hi - lo + 1) // 2) as m:
        for s in range(2):
            step(m * 2 + (lo + s), (lo + s) % 2)
    for i in range(hi + 1, last + 1):
        step(i, i % 2)


def has(b):
    return not isinstance(b, int) or 0 <= b < B


def blocks_of(v):
    full = ((v >> 1) & 31).with_bounds(min_val=1, max_val=B * S // BLK)
    return full, v & 1, v >> 6


def experts(eng, tab, expert):
    def pair(e, last):
        v = [eng.value_load(tab[0:1, bass.ds(e + half, 1)], min_val=2, max_val=64 * 64 - 1) for half in range(2)]
        for half in range(2):
            expert(e + half, half, not (last and half), *blocks_of(v[half]))

    with eng.Fori(0, E // 2 - 1) as m:
        pair(m * 2, False)
    pair(E - 2, True)


def adaln_moe_kernel(nc, x, modc_in, modb_in, attp, cst, we, out):
    _, CW = constants()
    ctx = ExitStack()
    with ctx:
        def sb(name, shape, dt=F32, stack=ctx):
            return stack.enter_context(nc.sbuf_tensor(name, shape, dt))

        def sem(name):
            return ctx.enter_context(nc.semaphore(name))

        modscr = nc.dram_tensor("modscr", [B, 4 * D], F32, kind="Internal").ap()
        gbscr = nc.dram_tensor("gbscr", [B, D], F32, kind="Internal").ap()
        xg = nc.dram_tensor("xg", [E * CAP, RW], F32, kind="Internal").ap()

        C = sb("C", [P, sum(n for _, n in CW.values())])
        whi = [sb("whi0", [P, NCH * WC], F32R), None]
        wlo = [sb("wlo0", [P, NCH * WC], F32R), None]
        raw = sb("raw", [P, NCH * WC])
        base = sb("base", [P, E])
        spare = sb("spare", [P, E])
        tabf = sb("tabf", [P, 4, E])
        tabi = sb("tabi", [P, E], I32)
        tab = sb("tab", [P, 3 * E + 1], I32)
        padt = sb("padt", [P, 1, RW])

        def c(name):
            a, n = CW[name]
            return C[:, a:a + n]

        att = ExitStack()
        X = sb("X", [P, B * NJ * D], stack=att)
        M1 = sb("M1", [P, sum(MODC.values())], stack=att)
        M2 = sb("M2", [P, sum(MODB.values())], stack=att)
        A1 = sb("A1", [P, sum(ATTP.values())], stack=att)
        sT = sb("sT", [P, KH, B], stack=att)
        sT1 = sb("sT1", [P, KH, B], stack=att)
        sT2 = sb("sT2", [P, KH, B], stack=att)
        modc = sb("modc", [P, 2, KH, B], stack=att)
        modr = sb("modr", [B, 5, D], stack=att)
        modb = [sb(f"modb{q}", [P, 4, D], stack=att) for q in range(2)]
        xn = sb("xn", [P, NJ, D], stack=att)
        hT = sb("hT", [P, KH, S], stack=att)
        hTh = sb("hTh", [P, KH, S], F32R, stack=att)
        hTl = sb("hTl", [P, KH, S], F32R, stack=att)
        wqh = sb("wqh", [P, KH, 3 * D], F32R, stack=att)
        wql = sb("wql", [P, KH, 3 * D], F32R, stack=att)
        qT = sb("qT", [P, KH, S], stack=att)
        bd = sb("bd", [P, KH, P], stack=att)
        gT = sb("gT", [P, KH, S], stack=att)
        modt = gT[0:B, :, :].rearrange("p k (a d) -> p k a d", a=2)
        owg = sb("owg", [P, KH, D], stack=att)
        h2 = [sb(f"h2{q}", [P, NJ, RW], stack=att) for q in range(2)]
        h2T = hT
        st1 = sb("st1", [P, NJ, 6], stack=att)
        mv1 = sb("mv1", [P, NJ, 2], stack=att)
        ve1 = sb("ve1", [P, NJ], stack=att)
        rs1 = sb("rs1", [P, NJ], stack=att)
        st2 = sb("st2", [P, NJ, 6], stack=att)
        mv2 = sb("mv2", [P, NJ, 2], stack=att)
        ve2 = sb("ve2", [P, NJ], stack=att)
        rs2 = sb("rs2", [P, NJ], stack=att)
        stc = sb("stc", [P, KH, 6], stack=att)
        mvc = sb("mvc", [P, KH, 2], stack=att)
        msq = sb("msq", [P, KH], stack=att)
        chst = sb("chst", [P, 2, KH], stack=att)
        gst = sb("gst", [P, 2, KH], stack=att)
        gnt = sb("gnt", [P, 6, KH], stack=att)
        gns = sb("gns", [P, 2, KH], stack=att)
        nm1 = sb("nm1", [P, 2, NJ], stack=att)
        nm2 = sb("nm2", [P, 2, NJ], stack=att)
        lgT = sb("lgT", [E, S], stack=att)
        lg = sb("lg", [P, NJ, E], stack=att)
        alg = sb("alg", [P, NJ, E], stack=att)
        mx = sb("mx", [P, NJ, 8], stack=att)
        ix = sb("ix", [P, NJ, 8], U32, stack=att)
        ixf = sb("ixf", [P, 2, NJ], stack=att)
        dl = sb("dl", [P, 2, NJ, E], stack=att)
        fc = sb("fc", [P, 2, NJ, E], stack=att)
        un = sb("un", [P, 2, NJ, E], stack=att)
        dc = sb("dc", [P, 2, NJ, E], stack=att)
        ex = sb("ex", [P, 2, NJ, E], stack=att)
        eu = sb("eu", [P, 2, NJ, E], stack=att)
        oh = sb("oh", [P, 2, NJ, E], stack=att)
        sm = sb("sm", [P, 2 * NJ], stack=att)
        wk = sb("wk", [P, 2 * NJ], stack=att)
        wt = sb("wt", [P, 2, NJ, E], stack=att)
        mk = sb("mk", [P, NJ * E], BF16, stack=att)
        trib = sb("trib", [P, 2 * P], BF16, stack=att)
        tokf = sb("tokf", [P, 2 * NJ], stack=att)
        slf = sb("slf", [P, NJ, E], stack=att)
        ssel = sb("ssel", [P, 2, NJ, E], stack=att)
        srow = sb("srow", [P, 2 * NJ], stack=att)
        slot = [sb(f"slot{q}", [P, 2 * NJ], I32, stack=att) for q in range(2)]
        kv = sb("kv", [P, NJ, 2 * D], stack=att)
        slot_last = sb("slot_last", [P, 2 * NJ], I32, stack=att)
        att.close()

        whi[1] = sb("whi1", [P, NCH * WC], F32R)
        wlo[1] = sb("wlo1", [P, NCH * WC], F32R)
        rows = sb("rows", [P, NT, D])
        meta = sb("meta", [P, NT, RW - D])
        xhi = sb("xhi", [P, KH, BLK], F32R)
        xlo = sb("xlo", [P, KH, BLK], F32R)
        sg = sb("sg", [P, 2, BLK])
        hf = sb("hf", [P, NF, BLK])
        hhi = sb("hhi", [P, NF, BLK], F32R)
        hlo = sb("hlo", [P, NF, BLK], F32R)
        gbr = sb("gbr", [P, NT, D])
        ysb = sb("ysb", [P, NT, D])

        ps = [ctx.enter_context(nc.psum_tensor(f"ps{i}", [P, 512], F32)) for i in range(8)]

        c_ld, mc_ld, mr_ld, a_ld = sem("c_ld"), sem("mc_ld"), sem("mr_ld"), sem("a_ld")
        x_ld = [sem(f"x_ld{n}") for n in range(4)]
        raw_ld = sem("raw_ld")
        mc_exp, mc_sil, mc_ps, mc_v, mc_st, mb_ld = (sem(n) for n in ("mc_exp", "mc_sil", "mc_ps", "mc_v", "mc_st", "mb_ld"))
        ini, held = sem("ini"), sem("held")
        ln1_l, bn1, r1l, r1, xn_r = (sem(n) for n in ("ln1_l", "bn1", "r1l", "r1", "xn_r"))
        wq_h, wq_l, hTf_r, hTl_r = (sem(n) for n in ("wq_h", "wq_l", "hTf_r", "hTl_r"))
        t1_ps, hT_r, q_ps, qT_r, kv_ps, kv_r, ktv_ps, bd_r = (
            sem(n) for n in ("t1_ps", "hT_r", "q_ps", "qT_r", "kv_ps", "kv_r", "ktv_ps", "bd_r"))
        c_ps, cs_l, cs_r, g_ps, g_cp, gn_l, gn_r, gT_r, owg_r = (
            sem(n) for n in ("c_ps", "cs_l", "cs_r", "g_ps", "g_cp", "gn_l", "gn_r", "gT_r", "owg_r"))
        gaob, o_ps, x1_r, x1_st = (sem(n) for n in ("gaob", "o_ps", "x1_r", "x1_st"))
        ln2_l, bn2, r2l, r2, xn2_r, md_l, h2_r = (sem(n) for n in ("ln2_l", "bn2", "r2l", "r2", "xn2_r", "md_l", "h2_r"))
        t2_ps, h2T_r, lT_ps, lT_r, l_ps, ro_l, dc_r, ex_r, mk_r, r_ps, rp_l, sl_r, scat = (
            sem(n) for n in ("t2_ps", "h2T_r", "lT_ps", "lT_r", "l_ps", "ro_l", "dc_r", "ex_r", "mk_r", "r_ps", "rp_l", "sl_r", "scat"))
        short_r = sem("short_r")
        scat_end = [sem(f"scat_end{n}") for n in range(2)]
        wp_h, wp_l = sem("wp_h"), sem("wp_l")
        tb_l, tab_r, pad_r, pad_st = (sem(n) for n in ("tb_l", "tab_r", "pad_r", "pad_st"))
        row_ld, tp_ps, xh_r, xT_r, gu_ps, sg_r, hf_r, hi_r, hs_r = (
            sem(n) for n in ("row_ld", "tp_ps", "xh_r", "xT_r", "gu_ps", "sg_r", "hf_r", "hi_r", "hs_r"))
        y_ps, y_r, gb_ld, add_st, mt_ld = (sem(n) for n in ("y_ps", "y_r", "gb_ld", "add_st", "mt_ld"))

        def part(tile, table, name):
            at = 0
            for n, w in table.items():
                if n == name:
                    return tile[:, at:at + w]
                at += w
            raise KeyError(name)

        cT = part(M1, MODC, "cT").rearrange("p (k b) -> p k b", k=KH)
        ob = part(M2, MODB, "ob")
        wmodc = part(M1, MODC, "wmodc").rearrange("p (k n) -> p k n", k=KH)
        wmodb = part(M2, MODB, "wmodb").rearrange("p (k n) -> p k n", k=KH)
        wqkv = part(A1, ATTP, "wqkv").rearrange("p (k n) -> p k n", k=KH)
        bkv = part(A1, ATTP, "bkv")
        ow = part(A1, ATTP, "ow").rearrange("p (k n) -> p k n", k=KH)
        gate = part(A1, ATTP, "gate").rearrange("p (k n) -> p k n", k=KH)
        bq, gnw, gnb = (part(A1, ATTP, n) for n in ("bq", "gnw", "gnb"))
        ident = c("ident")
        h2_last = kv[:, :, :].rearrange("p a b -> p (a b)")[:, 0:NJ * RW].rearrange("p (a b) -> p a b", a=NJ)

        def routed_rows(b, q):
            return h2_last if isinstance(b, int) and b == B - 1 else h2[q]

        def xb(b, off=0, n=NJ * D):
            return X[:, bass.ds(b * (NJ * D) + off, n)]

        def split(ap, **kw):
            return ap.rearrange("p (a b) -> p a b", **kw)

        def flat(tile):
            return tile[:, :, :, :].rearrange("p a b c -> p (a b c)")

        def hold(eng, s, value):
            if not (isinstance(value, int) and value <= 0):
                eng.wait_ge(s, value)
                eng.sem_inc(held, 1)

        def linker(eng, s, b, per, wait_ge=lambda eng, s, v: eng.wait_ge(s, v)):
            n = [0]

            def link(ins):
                n[0] += 1
                assert n[0] <= per
                ins.then_inc(s, 1)
                wait_ge(eng, s, b * per + n[0])
            return link

        def load_chunk(eng, e, n):
            eng.dma_start(raw[:, n * WC:(n + 1) * WC],
                          we[bass.ds(e, 1), :, n * WC:(n + 1) * WC].rearrange("o p n -> (o p) n")).then_inc(raw_ld, 16)

        def slots(b, q):
            return slot_last if isinstance(b, int) and b == B - 1 else slot[q]

        def pad(eng, e):
            first = eng.value_load(tab[0:1, bass.ds(e + 2 * E, 1)], min_val=0, max_val=E * CAP - BLK)
            eng.dma_start(xg[bass.ds(first, BLK), :].rearrange("(p t) d -> p t d", t=NT),
                          padt[:, :, :].broadcast_to([P, NT, RW])).then_inc(pad_st, 16)

        def residual(eng, i, q):
            hold(eng, mb_ld, i * 16 + 16)
            eng.tensor_tensor(split(xb(i), a=NJ), split(xb(i), a=NJ),
                              modb[q][:, 1:2, :].broadcast_to([P, NJ, D]), ALU.add).then_inc(gaob, 1)

        block = ctx.enter_context(nc.Block())

        @block.sync
        def _(sp):
            xv = x.rearrange("(b p j) d -> p b (j d)", p=P, j=NJ)
            Xv = X[:, :].rearrange("p (b n) -> p b n", b=B)
            ov = out.rearrange("(b p j) d -> b p (j d)", p=P, j=NJ)
            sp.dma_start(M1[:, :], modc_in).then_inc(mc_ld, 16)
            sp.dma_start(Xv[:, 0:1, :], xv[:, 0:1, :]).then_inc(x_ld[0], 16)
            sp.dma_start(C[:, :], cst).then_inc(c_ld, 16)
            sp.dma_start(A1[:, :], attp).then_inc(a_ld, 16)
            sp.dma_start(M2[:, :], modb_in).then_inc(mr_ld, 16)
            for n, (lo, hi) in ((1, (1, 2)), (2, (2, 3)), (3, (3, B))):
                sp.dma_start(Xv[:, lo:hi, :], xv[:, lo:hi, :]).then_inc(x_ld[n], 16)
            sp.wait_ge(mc_v, 12)
            sp.dma_start(modscr, modr[:, 0:4, :]).then_inc(mc_st, 16)
            sp.dma_start(gbscr, modr[:, 4, :]).then_inc(mc_st, 16)
            sp.wait_ge(mc_st, 32)

            def load_mod(b, q):
                sp.dma_start(modb[q][:, :, :].rearrange("p a n -> p (a n)"),
                             modscr[bass.ds(b, 1), :].broadcast_to([P, 4 * D])).then_inc(mb_ld, 16)

            load_mod(0, 0)
            sp.wait_ge(mb_ld, 16)
            load_mod(1, 1)
            for n in range(NCH):
                load_chunk(sp, 0, n)

            def store(b, q):
                hold(sp, x1_r, b * 2 + 2)
                sp.dma_start(ov[bass.ds(b, 1), :, :].rearrange("o p n -> (o p) n"), xb(b)).then_inc(x1_st, 16)

            def step(b, q):
                hold(sp, mb_ld, b * 16 + 32)
                hold(sp, h2_r, b + 1)
                load_mod(b + 2, q)
                store(b, q)

            steps(sp, step, 0, B - 3, 0, B - 3)

            store(B - 2, 0)
            store(B - 1, 1)

            def refill(lo, hi):
                for n in range(lo, hi):
                    sp.wait_ge(wp_l, n + 1)
                    load_chunk(sp, 1, n)

            def load_rows(first, g):
                hold(sp, tp_ps, g + 1)
                sp.dma_start(rows[:, :, :], xg[bass.ds(first, BLK), 0:D].rearrange("(t p) d -> p t d", t=NT))\
                  .then_inc(row_ld, 16)

            refill(0, NCH - 2)
            sp.wait_ge(short_r, 1)
            short = sp.value_load(tab[0:1, 3 * E:3 * E + 1], min_val=0, max_val=1)
            sp.wait_ge(scat, 16 + 128 * (B - 2))
            with sp.If(short < 1):
                load_rows(0, 0)
            sp.wait_ge(pad_r, 1)
            pad(sp, 0)
            with sp.If(short > 0):
                for s in scat_end:
                    sp.wait_ge(s, 128)
                sp.wait_ge(pad_st, 16)
                load_rows(0, 0)
            refill(NCH - 2, NCH)
            sp.wait_ge(tab_r, 1)

            def expert(e, half, more, full, tail, g0):
                for s in scat_end:
                    sp.wait_ge(s, 128)
                hold(sp, pad_st, e * 16 + 16)
                n = full + tail
                if more:
                    pad(sp, e + 1)
                with sp.If(n > 1):
                    with sp.Fori(1, n) as k:
                        load_rows(e * CAP + k * BLK, g0 + k)
                if more:
                    hold(sp, pad_st, e * 16 + 32)
                    load_rows((e + 1) * CAP, g0 + n)
                else:
                    load_rows(0, g0 + n)
                    hold(sp, row_ld, (g0 + n) * 16 + 16)
                    hold(sp, add_st, (g0 + n) * 32)

            experts(sp, tab, expert)

        @block.tensor
        def _(pe):
            pe.wait_ge(mc_ld, 16)
            pe.wait_ge(mc_sil, 3)
            for n, ch in enumerate((1, 0)):
                for h in range(KH):
                    for k in range(KH):
                        mm = pe.matmul(ps[6][:, (n * KH + h) * B:(n * KH + h + 1) * B],
                                       wmodc[:, k, ch * D + h * P:ch * D + (h + 1) * P], sT[:, k, :],
                                       start=(k == 0), stop=(k == KH - 1))
            mm.then_inc(mc_ps, 1)
            pe.wait_ge(c_ld, 16)
            pe.wait_ge(a_ld, 16)

            def step(i, q):
                cur, nxt, prv, old = has(i), has(i + 1), has(i - 1), has(i - 2)
                if nxt:
                    pe.wait_ge(xn_r, i + 2)
                    for h in range(KH):
                        for j in range(NJ):
                            mm = pe.transpose(ps[h][:, j * P:(j + 1) * P], xn[:, j, h * P:(h + 1) * P], ident)
                        mm.then_inc(t1_ps, 1)
                if old:
                    hold(pe, lT_r, i - 1)
                    for j in range(NJ):
                        mm = pe.transpose(ps[6][:, 256 + j * E:256 + (j + 1) * E], lgT[:, j * P:(j + 1) * P],
                                          C[0:E, CW["ident"][0]:CW["ident"][0] + E])
                    mm.then_inc(l_ps, 1)
                if cur:
                    pe.wait_ge(qT_r, i * 2 + 2)
                    wait(pe, x1_r, i * 2)
                    for h in range(KH):
                        pe.matmul(ps[2 + h][:, :], bd[:, h, :], qT[:, h, :], start=True, stop=True).then_inc(c_ps, 1)
                if isinstance(i, int) and i == -1:
                    pe.wait_ge(mr_ld, 16)
                    for n, ch in enumerate((2, 4, 3, 5)):
                        for k in range(KH):
                            mm = pe.matmul(ps[2 + n // 2][0:B, n % 2 * D:(n % 2 + 1) * D], sT[:, k, :],
                                           wmodb[:, k, (ch - 2) * D:(ch - 1) * D], start=(k == 0), stop=(k == KH - 1))
                    mm.then_inc(mc_ps, 1)
                    pe.wait_ge(ini, 1)
                    pe.wait_ge(wq_l, 1)
                if nxt:
                    for n, (w, h_) in enumerate(((wqh, hTh), (wql, hTh), (wqh, hTl))):
                        for m in range(KH):
                            for k in range(KH):
                                if m == 0 and h_ is hTl:
                                    pe.wait_ge(hTl_r, (i + 1) * 2 + k + 1)
                                elif m == 0 and n == 0:
                                    pe.wait_ge(hT_r, (i + 1) * 2 + k + 1)
                                mm = pe.matmul(ps[4 + m][:, :], w[:, k, m * P:(m + 1) * P], h_[:, k, :],
                                               start=(n == 0 and k == 0), stop=(n == 2 and k == KH - 1))
                            if n == 2:
                                mm.then_inc(q_ps, 1)

                def ranks():
                    pe.wait_ge(mk_r, i - 1)
                    for j in range(NJ + 1):
                        o = ps[7][:, 64 + j * E:64 + (j + 1) * E]
                        for n in range(min(j + 1, NJ)):
                            mm = pe.matmul(o, trib[:, P:2 * P] if n < j else trib[:, 0:P], mk[:, n * E:(n + 1) * E],
                                           start=(n == 0), stop=(n == min(j, NJ - 1)))
                    mm.then_inc(r_ps, 1)
                def averages():
                    pe.wait_ge(cs_r, i + 1)
                    pe.matmul(ps[6][:, 0:2 * KH], c("avg"), chst[:, :, :].rearrange("p a b -> p (a b)"),
                              start=True, stop=True).then_inc(g_ps, 1)

                if cur and not nxt:
                    averages()
                if old and not nxt:
                    ranks()
                if nxt:
                    for j in range(NJ):
                        if old and j == RAT:
                            ranks()
                        if cur and j == GAT:
                            averages()
                        if j == 0:
                            pe.wait_ge(hTf_r, (i + 1) * 2 + 2)
                        if j >= 2:
                            pe.wait_ge(qT_r, (i + 1) * 2 + j - 1)
                        for n, (h_, w) in enumerate(((hTh, wqh), (hTh, wql), (hTl, wqh))):
                            for k in range(KH):
                                mm = pe.matmul(ps[(0, 1, 4, 5)[j]][:, :], h_[:, k, j * P:(j + 1) * P],
                                               w[:, k, D:3 * D], start=(n == 0 and k == 0), stop=(n == 2 and k == KH - 1))
                        mm.then_inc(kv_ps, 1)
                    wait(pe, g_cp, i + 1)
                    for h in range(KH):
                        for j in range(NJ):
                            if h == 0:
                                pe.wait_ge(kv_r, (i + 1) * NJ + j + 1)
                            mm = pe.matmul(ps[6][:, h * P:(h + 1) * P], kv[:, j, h * P:(h + 1) * P],
                                           kv[:, j, D + h * P:D + (h + 1) * P], start=(j == 0), stop=(j == NJ - 1))
                    mm.then_inc(ktv_ps, 1)
                def project(n):
                    for j in (2 * n, 2 * n + 1):
                        for k in range(KH):
                            mm = pe.matmul(ps[2 + n][:, j % 2 * D:(j % 2 + 1) * D], gT[:, k, j * P:(j + 1) * P],
                                           owg[:, k, :], start=(k == 0), stop=(k == KH - 1))
                    mm.then_inc(o_ps, 1)

                if cur:
                    pe.wait_ge(gT_r, i * 2 + 2)
                    pe.wait_ge(owg_r, i + 1)
                    project(0)
                    if not nxt:
                        project(1)
                if prv:
                    pe.wait_ge(h2_r, i)
                    for h in range(KH):
                        for j in range(NJ):
                            mm = pe.transpose(ps[h][:, j * P:(j + 1) * P], routed_rows(i - 1, 1 - q)[:, j, h * P:(h + 1) * P], ident)
                        mm.then_inc(t2_ps, 1)
                if cur and nxt:
                    project(1)
                if nxt:
                    pe.wait_ge(bd_r, i + 2)
                if prv:
                    for k in range(KH):
                        pe.wait_ge(h2T_r, (i - 1) * 2 + k + 1)
                        mm = pe.matmul(ps[6][0:E, :], gate[:, k, :], h2T[:, k, :], start=(k == 0), stop=(k == KH - 1))
                    mm.then_inc(lT_ps, 1)

            steps(pe, step, -1, B + 1, 2, B - 3)

            def turn(g):
                pe.wait_ge(row_ld, g * 16 + 16)
                for k in range(KH):
                    for t in range(NT):
                        mm = pe.transpose(ps[7][:, k * BLK + t * P:k * BLK + (t + 1) * P], rows[:, t, k * P:(k + 1) * P],
                                          ident)
                mm.then_inc(tp_ps, 1)

            def expert(e, half, more, full, tail, g0):
                hi, lo = whi[half], wlo[half]
                hold(pe, wp_l, (e + 1) * NCH)

                def up(g, f):
                    pe.wait_ge(hf_r, g * NF + f + 1)
                    for n_, o in enumerate((0, BLK)):
                        for a, b_ in ((hi, xhi), (lo, xhi), (hi, xlo)):
                            if f == 0 and n_ == 0 and b_ is xlo:
                                pe.wait_ge(xT_r, g + 1)
                            for k in range(KH):
                                at = (n_ * KH + k) * F + f * P
                                mm = pe.matmul(ps[f % 4][:, o:o + BLK], a[:, at:at + P], b_[:, k, :],
                                               start=(k == 0 and a is hi and b_ is xhi),
                                               stop=(k == KH - 1 and b_ is xlo))
                    mm.then_inc(gu_ps, 1)

                def down(g, f):
                    pe.wait_ge(hs_r, g * NF + f + 1)
                    if f == 0:
                        pe.wait_ge(y_r, g + 1)
                    at = (2 * KH * F) + f * D
                    for t in range(NT):
                        for a, b_ in ((hhi, hi), (hlo, hi), (hhi, lo)):
                            mm = pe.matmul(ps[4 + t][:, 0:D], a[:, f, t * P:(t + 1) * P], b_[:, at:at + D],
                                           start=(f == 0 and a is hhi and b_ is hi),
                                           stop=(f == NF - 1 and b_ is lo))
                    if f == NF - 1:
                        mm.then_inc(y_ps, 1)

                def hidden(g, c_, n):
                    pe.wait_ge(hf_r, g * NF + c_ * NTF + NTF + 4)
                    for j in range(NTF):
                        mm = pe.transpose(ps[2 * c_][:, j * P:(j + 1) * P],
                                          hf[:, 2 * c_ + j // NT, j % NT * P:(j % NT + 1) * P], ident)
                    mm.then_inc(gu_ps, n)

                def tail_block(g):
                    pe.wait_ge(xh_r, g + 1)
                    pe.wait_ge(xT_r, g + 1)
                    pe.wait_ge(hf_r, g * NF + 4)
                    for c_ in range(2):
                        for n_ in range(2):
                            for a, b_ in ((xhi, hi), (xhi, lo), (xlo, hi)):
                                for k in range(KH):
                                    at = (n_ * KH + k) * F + c_ * NTF * P
                                    mm = pe.matmul(ps[2 * c_ + n_][:, :], a[:, k, 0:P], b_[:, at:at + NTF * P],
                                                   start=(k == 0 and a is xhi and b_ is hi),
                                                   stop=(k == KH - 1 and a is xlo))
                            mm.then_inc(gu_ps, 1)
                            if c_ == 1 and n_ == 0:
                                hidden(g, 0, 1)
                    turn(g + 1)
                    for f in range(NF):
                        if f == 1:
                            hidden(g, 1, NF - 5)
                        if f % NTF == 0:
                            pe.wait_ge(hs_r, g * NF + f + NTF)
                        if f == 0:
                            pe.wait_ge(y_r, g + 1)
                        at = (2 * KH * F) + f * D
                        for a, b_ in ((hhi, hi), (hlo, hi), (hhi, lo)):
                            mm = pe.matmul(ps[4][:, 0:D], a[:, f, 0:P], b_[:, at:at + D],
                                           start=(f == 0 and a is hhi and b_ is hi),
                                           stop=(f == NF - 1 and b_ is lo))
                    mm.then_inc(y_ps, 1)

                with pe.Fori(0, full) as k_:
                    g = g0 + k_
                    pe.wait_ge(xh_r, g + 1)
                    for f in range(NF):
                        if f == NF - 1:
                            turn(g + 1)
                        up(g, f)
                        if f >= LAG:
                            down(g, f - LAG)
                    for f in range(NF - LAG, NF):
                        down(g, f)
                with pe.If(tail > 0):
                    tail_block(g0 + full)

            pe.wait_ge(sl_r, B)
            turn(0)
            pe.wait_ge(tab_r, 1)
            experts(pe, tab, expert)

        @block.scalar
        def _(act):
            act.wait_ge(mc_ld, 16)
            act.activation(sT1[:, :, :], cT, ACT.Exp, scale=-1.0).then_inc(mc_exp, 1)

            def norm(b, src, dst, mv_, nm_, rs_, ready):
                act.wait_ge(ready, b + 1)
                for j in range(NJ):
                    ins = act.activation(dst(j), src(b, j * D, D), ACT.Identity, bias=nm_[:, 1, j:j + 1],
                                         scale=rs_[:, j:j + 1])
                return ins

            def second_norm(b, q):
                rows_ = routed_rows(b, 1 - q)
                norm(b, xb, lambda j: rows_[:, j, 0:D], mv2, nm2, rs2, r2).then_inc(xn2_r, 1)

            def first_norm(b):
                wait(act, t1_ps, b * 2)
                norm(b, xb, lambda j: xn[:, j, :], mv1, nm1, rs1, r1).then_inc(xn_r, 1)

            def high_weights(dst, chunk):
                act.activation(whi[dst][:, bass.ds(chunk * WC, WC)], raw[:, bass.ds(chunk * WC, WC)], ACT.Copy)\
                    .then_inc(wp_h, 1)

            def high_chunks(chunks):
                act.wait_ge(raw_ld, 16 * NCH)
                for n in chunks:
                    high_weights(0, n)

            def exponents(b):
                act.wait_ge(dc_r, b + 1)
                act.activation(flat(ex), flat(dc), ACT.Exp, scale=-1.0).then_inc(ex_r, 1)

            first_norm(0)
            act.wait_ge(a_ld, 16)
            act.activation(wqh[:, :, :], wqkv, ACT.Copy).then_inc(wq_h, 1)
            act.wait_ge(mc_v, 2)

            def step(i, q):
                cur, nxt, prv, old, nx2 = has(i), has(i + 1), has(i - 1), has(i - 2), has(i + 2)
                last = not nxt
                if nxt:
                    hold(act, hTl_r, (i + 1) * 2)
                    for dst, ready in ((hTh, hT_r), (hT, hTf_r)):
                        for h in range(KH):
                            if dst is hTh:
                                hold(act, t1_ps, (i + 1) * 2 + h + 1)
                            act.activation(dst[:, h, :], ps[h][:, :], ACT.Identity, bias=modc[:, 1, h, bass.ds(i + 1, 1)],
                                           scale=modc[:, 0, h, bass.ds(i + 1, 1)]).then_inc(ready, 1)
                if not cur and nx2:
                    first_norm(i + 2)
                if nxt:
                    for m in range(KH):
                        act.wait_ge(q_ps, (i + 1) * 2 + m + 1)
                        act.activation(qT[:, m, :], ps[4 + m][:, :], ACT.Identity, bias=bq[:, m:m + 1]).then_inc(qT_r, 1)
                if old and nxt:
                    exponents(i - 2)
                if prv:
                    if nxt:
                        wait(act, scat, 16 + (i - 2) * 128)
                        second_norm(i - 1, q)
                if last and i == B:
                    second_norm(B - 1, q)
                if old and not nxt:
                    exponents(i - 2)
                if last and i == B - 1:
                    high_chunks((0,))
                if last and i == B:
                    high_chunks((3, 4))
                if last and i == B + 1:
                    act.activation(spare[:, 7:8], c("ones")[:, 0:1], ACT.Silu)
                if cur:
                    act.wait_ge(gn_r, i + 1)
                    for h in range(KH):
                        act.activation(gT[:, h, :], ps[2 + h][:, :], ACT.Identity, bias=gns[:, 1, h:h + 1],
                                       scale=gns[:, 0, h:h + 1]).then_inc(gT_r, 1)
                if cur and nx2:
                    first_norm(i + 2)
                if last and i == B - 1:
                    wait(act, scat, 16 + (i - 2) * 128)
                    second_norm(i - 1, q)
                    high_chunks((1, 2))
                if prv:
                    for h in range(KH):
                        act.wait_ge(t2_ps, (i - 1) * 2 + h + 1)
                        act.activation(h2T[:, h, :], ps[h][:, :], ACT.Copy).then_inc(h2T_r, 1)
                if last and i == B:
                    high_chunks((5, 6))
                if prv:
                    act.wait_ge(lT_ps, i)
                    act.activation(lgT[:, :], ps[6][0:E, :], ACT.Copy).then_inc(lT_r, 1)
                if last and i == B:
                    high_chunks((7,))

            steps(act, step, -1, B + 1, 2, B - 3)

            act.wait_ge(sl_r, B)

            def turned(g):
                act.wait_ge(tp_ps, g + 2)
                act.activation(xhi[:, :, :].rearrange("p k n -> p (k n)"), ps[7][:, :], ACT.Copy).then_inc(xh_r, 1)

            turned(0)
            act.wait_ge(tab_r, 1)
            act.wait_ge(x1_st, 16 * B)

            def expert(e, half, more, full, tail, g0):

                def high(g, f):
                    act.wait_ge(hf_r, g * NF + f + 1 + 4)
                    act.activation(hhi[:, f, :], hf[:, f, :], ACT.Copy).then_inc(hi_r, 1)

                def refill(n):
                    if not isinstance(e, int):
                        hold(act, wp_l, (e + 1) * NCH + n + 1)
                        load_chunk(act, e + 2, n)

                def block_(g, first):
                    for f in range(NF):
                        if f:
                            high(g, f - 1)
                        act.wait_ge(gu_ps, g * NF + f + 1)
                        act.activation(sg[:, f % 2, :], ps[f % 4][:, 0:BLK], ACT.Silu).then_inc(sg_r, 1)
                        if first and more and f < NCH - 1:
                            if f == 0:
                                hold(act, raw_ld, (e + 2) * (16 * NCH))
                            high_weights(1 - half, f)
                            if f:
                                refill(f - 1)
                    turned(g + 1)
                    high(g, NF - 1)
                    if first and more:
                        high_weights(1 - half, NCH - 1)
                        refill(NCH - 2)
                        refill(NCH - 1)

                def tail_block(g):
                    def gate(c_, n, m):
                        act.wait_ge(gu_ps, g * NF + n)
                        act.activation(hf[:, NTF + 2 * c_:NTF + 2 * c_ + 2, :].rearrange("p a b -> p (a b)"), ps[2 * c_][:, :],
                                       ACT.Silu).then_inc(sg_r, m)

                    def high_half(c_, n):
                        act.wait_ge(gu_ps, g * NF + n)
                        act.activation(hhi[:, c_ * NTF:(c_ + 1) * NTF, 0:P], split(ps[2 * c_][:, :], a=NTF), ACT.Copy)\
                            .then_inc(hi_r, NTF)

                    gate(0, 1, 1)
                    gate(1, 3, NF - 1)
                    high_half(0, 4)
                    turned(g + 1)
                    high_half(1, NF)

                block_(g0, True)
                with act.If(full > 1):
                    with act.Fori(1, full) as k:
                        block_(g0 + k, False)
                with act.If(tail > 0):
                    tail_block(g0 + full)

            experts(act, tab, expert)

        @block.vector
        def _(dve):
            dve.wait_ge(mc_exp, 1)
            dve.tensor_scalar(sT2[:, :, :], sT1[:, :, :], 1.0, None, ALU.add).then_inc(mc_sil, 1)
            dve.wait_ge(mc_sil, 1)
            dve.reciprocal(sT1[:, :, :], sT2[:, :, :]).then_inc(mc_sil, 1)
            dve.wait_ge(mc_sil, 2)
            dve.tensor_tensor(sT[:, :, :], sT1[:, :, :], cT, ALU.mult).then_inc(mc_sil, 1)

            def layer_stats(b, src, stt_, mv, nm, l, read, out_sem):
                for j in range(NJ):
                    ins = dve.bn_stats(stt_[:, j, :], src(b, j * D, D))
                ins.then_inc(l, 1)
                hold(dve, read, b)
                hold(dve, l, b * 2 + 1)
                for j in range(NJ):
                    ins = dve.bn_aggr(mv[:, j, :], stt_[:, j, :])
                ins.then_inc(l, 1)
                hold(dve, l, b * 2 + 2)
                dve.tensor_scalar(nm[:, 0, :], mv[:, :, 0], -1.0, None, ALU.mult).then_inc(out_sem, 1)

            def first_stats(b):
                if isinstance(b, int):
                    dve.wait_ge(x_ld[min(b, 3)], 16)
                layer_stats(b, xb, st1, mv1, nm1, ln1_l, r1, bn1)

            first_stats(0)
            dve.wait_ge(mc_ps, 1)
            dve.tensor_scalar(modc[:, 0, :, :], split(ps[6][:, 0:KH * B], a=KH), 1.0, None, ALU.add).then_inc(mc_v, 1)
            dve.tensor_copy(modc[:, 1, :, :], split(ps[6][:, KH * B:2 * KH * B], a=KH)).then_inc(mc_v, 1)
            dve.wait_ge(c_ld, 16)
            dve.memset(padt[:, :, 0:TOK], 0.0)
            dve.memset(padt[:, :, BAT:BAT + 1], 0.0)
            dve.memset(padt[:, :, TOK:TOK + 1].bitcast(I32), NOROW)
            dve.tensor_copy(trib[:, :], C[:, CW["before"][0]:CW["before"][0] + 2 * P]).then_inc(ini, 1)
            dve.tensor_copy(tokf[:, :], c("token")).then_inc(ini, 1)
            dve.wait_ge(ini, 2)
            dve.wait_ge(scat, 16)
            dve.wait_ge(a_ld, 16)
            dve.wait_ge(wq_h, 1)
            dve.tensor_tensor(wql[:, :, :], wqkv, wqh[:, :, :].bitcast(F32), ALU.subtract).then_inc(wq_l, 1)

            def modulation_rows():
                dve.wait_ge(mc_ps, 2)
                g2 = (ps[2][0:B, 0:D], ps[3][0:B, D:2 * D])
                for n in range(2):
                    dve.tensor_scalar(modt[:, n, 0, :], g2[n], 0.0, None, ALU.is_ge).then_inc(mc_v, 1)
                    dve.tensor_scalar(modt[:, n, 1, :], g2[n], -1.0, None, ALU.mult).then_inc(mc_v, 1)
                dve.wait_ge(mc_v, 6)
                for n in range(2):
                    dve.tensor_scalar(modt[:, n, 0, :], modt[:, n, 0, :], 2.0, -1.0, ALU.mult, ALU.add)
                    dve.scalar_tensor_tensor(modt[:, n, 1, :], modt[:, n, 1, :], 0.25, g2[n], ALU.max, ALU.max)\
                       .then_inc(mc_v, 1)
                dve.wait_ge(mc_v, 8)
                dve.tensor_tensor(modr[:, 0, :], modt[:, 0, 0, :], modt[:, 0, 1, :], ALU.mult).then_inc(mc_v, 1)
                dve.tensor_tensor(modr[:, 4, :], modt[:, 1, 0, :], modt[:, 1, 1, :], ALU.mult)
                dve.tensor_scalar(modr[:, 2, :], ps[2][0:B, D:2 * D], 1.0, None, ALU.add).then_inc(mc_v, 1)
                dve.tensor_copy(modr[:, 3, :], ps[3][0:B, 0:D]).then_inc(mc_v, 1)
                dve.wait_ge(mc_v, 9)
                dve.tensor_tensor(modr[:, 1, :], modr[:, 0, :], ob[0:B, :], ALU.mult).then_inc(mc_v, 1)

            def context_stats(i):
                link = linker(dve, cs_l, i, 3, hold)
                for h in range(KH):
                    dve.wait_ge(c_ps, i * 2 + h + 1)
                    ins = dve.bn_stats(stc[:, h, :], ps[2 + h][:, :])
                link(ins)
                for h in range(KH):
                    ins = dve.bn_aggr(mvc[:, h, :], stc[:, h, :])
                link(ins)
                dve.tensor_copy(chst[:, 0, :], mvc[:, :, 0])
                link(dve.tensor_tensor(msq[:, :], mvc[:, :, 0], mvc[:, :, 0], ALU.mult))
                dve.tensor_tensor(chst[:, 1, :], msq[:, :], mvc[:, :, 1], ALU.add).then_inc(cs_r, 1)

            def keep_kv(b, j):
                dve.wait_ge(kv_ps, b * NJ + j + 1)
                dve.tensor_tensor(kv[:, j, :], ps[(0, 1, 4, 5)[j]][:, :], bkv, ALU.add).then_inc(kv_r, 1)

            def keep_logits(b):
                dve.wait_ge(l_ps, b + 1)
                dve.tensor_copy(lg[:, :, :], split(ps[6][:, 256:256 + NJ * E], a=NJ)).then_inc(ro_l, 1)

            def two_best(b):
                dve.wait_ge(ro_l, b * 5 + 1)
                dve.scalar_tensor_tensor(alg[:, :, :], lg[:, :, :], -1.0, lg[:, :, :], ALU.mult, ALU.max)
                for j in range(NJ):
                    ins = dve.max(mx[:, j, :], lg[:, j, :])
                ins.then_inc(ro_l, 1)
                dve.wait_ge(ro_l, b * 5 + 2)
                for k in range(2):
                    best = mx[:, :, k:k + 1].broadcast_to([P, NJ, E])
                    dve.tensor_tensor(dl[:, k, :, :], best, lg[:, :, :], ALU.subtract)
                    dve.tensor_tensor(fc[:, k, :, :], best, alg[:, :, :], ALU.max)
                for j in range(NJ):
                    ins = dve.max_index(ix[:, j, :], mx[:, j, :], lg[:, j, :])
                ins.then_inc(ro_l, 1)

            def routing(b):
                dve.wait_ge(ro_l, b * 5 + 3)
                dve.tensor_copy(ixf[:, :, :], ix[:, :, 0:2].rearrange("p j k -> p k j"))
                dve.tensor_scalar(flat(dc), flat(dl), 0.0, None, ALU.max).then_inc(dc_r, 1)
                dve.scalar_tensor_tensor(flat(un), flat(fc), JITTER, flat(dl), ALU.mult, ALU.is_ge).then_inc(ro_l, 1)
                dve.wait_ge(ro_l, b * 5 + 4)
                for k in range(2):
                    ins = dve.tensor_tensor(oh[:, k, :, :], split(c("iota"), a=NJ),
                                            ixf[:, k, :].rearrange("p (j o) -> p j o", o=1).broadcast_to([P, NJ, E]),
                                            ALU.is_equal)
                ins.then_inc(ro_l, 1)
                dve.wait_ge(ro_l, b * 5 + 5)
                dve.scalar_tensor_tensor(un[:, 1, :, :], oh[:, 0, :, :], 0.5, un[:, 1, :, :], ALU.is_lt, ALU.mult)
                dve.tensor_tensor(split(mk[:, :], a=NJ), oh[:, 0, :, :], oh[:, 1, :, :], ALU.add).then_inc(mk_r, 1)

            def routed(b, q):
                link = linker(dve, rp_l, b, 4)
                dve.wait_ge(ex_r, b + 1)
                dve.wait_ge(mk_r, b + 1)
                dve.wait_ge(r_ps, b + 1)
                dve.tensor_tensor(flat(eu), flat(ex), flat(un), ALU.mult)
                link(dve.tensor_tensor(slf[:, :, :], split(ps[7][:, 64:64 + NJ * E], a=NJ),
                                       base[:, :].rearrange("p (o e) -> p o e", o=1).broadcast_to([P, NJ, E]), ALU.add))
                dve.tensor_reduce(sm[:, :], eu[:, :, :, :].rearrange("p a b c -> p (a b) c"), AX_X, ALU.add)
                for k in range(2):
                    dve.tensor_tensor(ssel[:, k, :, :], oh[:, k, :, :], slf[:, :, :], ALU.mult)
                dve.tensor_copy(routed_rows(b, q)[:, :, TOK:TOK + 2].bitcast(I32), split(tokf[:, :], a=NJ))
                link(dve.tensor_tensor(base[:, :], base[:, :], ps[7][:, 64 + NJ * E:64 + (NJ + 1) * E], ALU.add))
                dve.reciprocal(wk[:, :], sm[:, :])
                dve.tensor_tensor(tokf[:, :], tokf[:, :], c("step"), ALU.add)
                link(dve.tensor_reduce(srow[:, :], ssel[:, :, :, :].rearrange("p a b c -> p (a b) c"), AX_X, ALU.add))
                dve.tensor_copy(slots(b, q)[:, :], srow[:, :])
                link(dve.tensor_tensor(wt[:, :, :, :].rearrange("p a b c -> p (a b) c"),
                                       oh[:, :, :, :].rearrange("p a b c -> p (a b) c"),
                                       wk[:, :].rearrange("p (n o) -> p n o", o=1).broadcast_to([P, 2 * NJ, E]), ALU.mult))
                dve.tensor_tensor(routed_rows(b, q)[:, :, META:META + E], wt[:, 0, :, :], wt[:, 1, :, :], ALU.add).then_inc(sl_r, 1)
                if isinstance(b, int) and b == B - 3:
                    dve.tensor_scalar(tab[:, 3 * E:3 * E + 1], base[:, 0:1], float(BLK), None, ALU.is_lt).then_inc(short_r, 1)

            def low_weights(dst, chunk, n):
                dve.wait_ge(wp_h, n)
                return dve.tensor_tensor(wlo[dst][:, bass.ds(chunk * WC, WC)], raw[:, bass.ds(chunk * WC, WC)],
                                         whi[dst][:, bass.ds(chunk * WC, WC)].bitcast(F32), ALU.subtract)

            def keep_averages(i):
                dve.wait_ge(g_ps, i + 1)
                dve.tensor_copy(gst[:, :, :].rearrange("p a b -> p (a b)"), ps[6][:, 0:2 * KH]).then_inc(g_cp, 1)

            def low_chunk(n):
                low_weights(0, n, n + 1).then_inc(wp_l, 1)

            def step(i, q):
                cur, nxt, prv, old, nx2 = has(i), has(i + 1), has(i - 1), has(i - 2), has(i + 2)
                last = not nxt
                if prv:
                    layer_stats(i - 1, xb, st2, mv2, nm2, ln2_l, r2, bn2)
                if cur and nx2:
                    first_stats(i + 2)
                if nxt:
                    for h in range(KH):
                        dve.wait_ge(hTf_r, (i + 1) * 2 + h + 1)
                        dve.tensor_tensor(hTl[:, h, :], hT[:, h, :], hTh[:, h, :].bitcast(F32), ALU.subtract).then_inc(hTl_r, 1)
                if isinstance(i, int) and i == -1:
                    first_stats(i + 2)
                    modulation_rows()
                if old:
                    keep_logits(i - 2)
                if cur:
                    context_stats(i)
                if last and cur:
                    keep_averages(i)
                if old:
                    two_best(i - 2)
                if cur and nxt:
                    keep_averages(i)
                if old:
                    routing(i - 2)
                if last and cur:
                    residual(dve, i, q)
                if last and i == B + 1:
                    low_chunk(6)
                if last and i != B:
                    routed(i - 2, q)
                if last and cur:
                    low_chunk(0)
                if nxt:
                    for j in range(NJ):
                        keep_kv(i + 1, j)
                if prv:
                    dve.wait_ge(xn2_r, i)
                    h = routed_rows(i - 1, 1 - q)[:, :, 0:D]
                    dve.tensor_tensor(h, h, modb[1 - q][:, 2:3, :].broadcast_to([P, NJ, D]), ALU.mult).then_inc(md_l, 1)
                if nxt:
                    dve.wait_ge(ktv_ps, i + 2)
                    dve.tensor_tensor(bd[:, :, :].rearrange("p a b -> p (a b)"), ps[6][:, 0:KH * P], c("mask"), ALU.mult)\
                       .then_inc(bd_r, 1)
                if prv:
                    dve.wait_ge(md_l, i)
                    dve.tensor_tensor(h, h, modb[1 - q][:, 3:4, :].broadcast_to([P, NJ, D]), ALU.add).then_inc(h2_r, 1)
                if old and nxt or isinstance(i, int) and i == B:
                    routed(i - 2, q)
                if last and i == B:
                    for n in range(1, 6):
                        low_chunk(n)
                if cur:
                    dve.wait_ge(gaob, i + 1)
                    for n in range(2):
                        dve.wait_ge(o_ps, i * 2 + n + 1)
                        dve.tensor_tensor(xb(i, n * 2 * D, 2 * D), ps[2 + n][:, :], xb(i, n * 2 * D, 2 * D), ALU.add)\
                           .then_inc(x1_r, 1)
                    hold(dve, x1_r, i * 2 + 2)

            steps(dve, step, -1, B + 1, 2, B - 3)

            n_tab = [0]

            def tlink(ins):
                n_tab[0] += 1
                ins.then_inc(tb_l, 1)
                dve.wait_ge(tb_l, n_tab[0])

            dve.tensor_copy(tab[:, 2 * E:3 * E], base[:, :]).then_inc(pad_r, 1)
            tlink(dve.tensor_tensor(tabf[:, 0, :], base[:, :], c("region"), ALU.subtract))
            tlink(dve.tensor_scalar(tabf[:, 1, :], tabf[:, 0, :], float(P - 1), None, ALU.add))
            tlink(dve.tensor_copy(tabi[:, :], tabf[:, 1, :]))
            tlink(dve.tensor_scalar(tab[:, 0:E], tabi[:, :], P.bit_length() - 1, None, ALU.logical_shift_right))
            tlink(dve.tensor_copy(tabf[:, 2, :], tab[:, 0:E]))
            tlink(dve.tensor_scalar(tabf[:, 2, :], tabf[:, 2, :], float(NT), None, ALU.max))
            tlink(dve.tensor_scalar(tabf[:, 1, :], tabf[:, 2, :], float(NT - 1), None, ALU.add))
            tlink(dve.tensor_copy(tabi[:, :], tabf[:, 1, :]))
            tlink(dve.tensor_scalar(tab[:, 0:E], tabi[:, :], NT.bit_length() - 1, None, ALU.logical_shift_right))
            tlink(dve.tensor_copy(tabf[:, 3, :], tab[:, 0:E]))
            tlink(dve.tensor_tensor_scan(tabf[:, 0, :], c("ones")[:, 0:E], tabf[:, 3, :], 0.0, ALU.mult, ALU.add))
            tlink(dve.tensor_tensor(tabf[:, 1, :], tabf[:, 0, :], tabf[:, 3, :], ALU.subtract))
            dve.scalar_tensor_tensor(tab[:, 0:E], tabf[:, 1, :], 64.0, tabf[:, 2, :], ALU.mult, ALU.add).then_inc(tab_r, 1)
            low_chunk(NCH - 1)
            dve.wait_ge(tab_r, 1)
            dve.wait_ge(x1_st, 16 * B)

            def turned(g):
                dve.wait_ge(xh_r, g + 1)
                dve.tensor_tensor(xlo[:, :, :].rearrange("p k n -> p (k n)"), ps[7][:, :],
                                  xhi[:, :, :].rearrange("p k n -> p (k n)").bitcast(F32), ALU.subtract).then_inc(xT_r, 1)

            turned(0)

            def expert(e, half, more, full, tail, g0):

                def low(g, f):
                    dve.wait_ge(hi_r, g * NF + f + 1)
                    dve.tensor_tensor(hlo[:, f, :], hf[:, f, :], hhi[:, f, :].bitcast(F32), ALU.subtract)\
                       .then_inc(hs_r, 1)

                def block_(g, first):
                    for f in range(NF):
                        if f:
                            low(g, f - 1)
                        dve.wait_ge(sg_r, g * NF + f + 1)
                        dve.tensor_tensor(hf[:, f, :], ps[f % 4][:, BLK:2 * BLK], sg[:, f % 2, :], ALU.mult)\
                           .then_inc(hf_r, 1)
                        if first and more and f < NCH - 1:
                            low_weights(1 - half, f, (e + 1) * NCH + f + 1).then_inc(wp_l, 1)
                    low(g, NF - 1)
                    turned(g + 1)
                    if first and more:
                        low_weights(1 - half, NCH - 1, (e + 2) * NCH).then_inc(wp_l, 1)
                    gated(g, NT)

                def gated(g, tiles):
                    dve.wait_ge(gb_ld, g * 32 + 32)
                    dve.wait_ge(y_ps, g + 2)
                    for t in range(tiles):
                        ins = dve.scalar_tensor_tensor(ysb[:, t, :], ps[4 + t][:, 0:D], meta[:, t, bass.ds(e, 1)],
                                                       gbr[:, t, :], ALU.mult, ALU.mult)
                    ins.then_inc(y_r, 1)

                def tail_block(g):
                    def mult(c_, n, m):
                        dve.wait_ge(sg_r, g * NF + n)
                        dve.wait_ge(gu_ps, g * NF + m)
                        dve.tensor_tensor(hf[:, 2 * c_:2 * c_ + 2, :].rearrange("p a b -> p (a b)"), ps[2 * c_ + 1][:, :],
                                          hf[:, NTF + 2 * c_:NTF + 2 * c_ + 2, :].rearrange("p a b -> p (a b)"), ALU.mult)\
                           .then_inc(hf_r, NTF)

                    def low_half(c_):
                        dve.wait_ge(hi_r, g * NF + (c_ + 1) * NTF)
                        dve.tensor_tensor(hlo[:, c_ * NTF:(c_ + 1) * NTF, 0:P], split(ps[2 * c_][:, :], a=NTF),
                                          hhi[:, c_ * NTF:(c_ + 1) * NTF, 0:P].bitcast(F32), ALU.subtract).then_inc(hs_r, NTF)

                    mult(0, 1, 2)
                    low_half(0)
                    mult(1, NF, 5)
                    turned(g + 1)
                    low_half(1)
                    gated(g, 1)

                block_(g0, True)
                with dve.If(full > 1):
                    with dve.Fori(1, full) as k:
                        block_(g0 + k, False)
                with dve.If(tail > 0):
                    tail_block(g0 + full)

            experts(dve, tab, expert)

        @block.gpsimd
        def _(pool):
            pool.memset(spare[:, 0:1], 0.0).then_inc(hf_r, 4)
            pool.memset(spare[:, 1:2], 0.0).then_inc(y_r, 1)
            pool.memset(spare[:, 2:3], 0.0).then_inc(y_ps, 1)
            pool.memset(spare[:, 3:4], 0.0).then_inc(tp_ps, 1)

            pool.dma_start(base[:, :], cst[:, CW["region"][0]:CW["region"][0] + E]).then_inc(scat, 16)

            def rstd(b, mv, nm, ve, rs, ready, l, done, normed):
                hold(pool, ready, b + 1)
                hold(pool, done, b)
                hold(pool, normed, b)
                pool.tensor_scalar(ve[:, :], mv[:, :, 1], EPS, None, ALU.add).then_inc(l, 1)
                hold(pool, l, b * 2 + 1)
                pool.tensor_tensor(rs[:, :], ve[:, :], c("half"), ALU.pow).then_inc(l, 1)
                hold(pool, l, b * 2 + 2)
                pool.tensor_tensor(nm[:, 1, :], nm[:, 0, :], rs[:, :], ALU.mult).then_inc(done, 1)

            def group_norm(i):
                link = linker(pool, gn_l, i, 6, hold)
                hold(pool, g_cp, i + 1)
                link(pool.tensor_tensor(gnt[:, 0, :], gst[:, 0, :], gst[:, 0, :], ALU.mult))
                link(pool.tensor_tensor(gnt[:, 1, :], gst[:, 1, :], gnt[:, 0, :], ALU.subtract))
                link(pool.tensor_scalar(gnt[:, 2, :], gnt[:, 1, :], EPS, None, ALU.add))
                link(pool.tensor_tensor(gnt[:, 3, :], gnt[:, 2, :], c("half")[:, 0:KH], ALU.pow))
                link(pool.tensor_tensor(gns[:, 0, :], gnt[:, 3, :], gnw, ALU.mult))
                link(pool.tensor_tensor(gnt[:, 4, :], gst[:, 0, :], gns[:, 0, :], ALU.mult))
                pool.tensor_tensor(gns[:, 1, :], gnb, gnt[:, 4, :], ALU.subtract).then_inc(gn_r, 1)

            def scatter(b, q, lo=0, hi=2 * NJ):
                hold(pool, sl_r, b + 1)
                for n in range(lo, hi):
                    pool.indirect_dma_start(xg, bass.IndirectOffsetOnAxis(ap=slots(b, q)[:, n:n + 1], axis=0),
                                            routed_rows(b, q)[:, n % NJ, :], None)\
                        .then_inc(scat_end[b - (B - 2)] if isinstance(b, int) and b >= B - 2 else scat, 16)

            def second_rstd(b):
                rstd(b, mv2, nm2, ve2, rs2, bn2, r2l, r2, xn2_r)

            def step(i, q):
                cur, nxt, prv, old, nx2 = has(i), has(i + 1), has(i - 1), has(i - 2), has(i + 2)
                if prv and nxt:
                    second_rstd(i - 1)
                if cur:
                    group_norm(i)
                    hold(pool, mb_ld, i * 16 + 16)
                    pool.tensor_tensor(owg[:, :, :], ow, modb[q][:, 0:1, :].broadcast_to([P, KH, D]), ALU.mult)\
                        .then_inc(owg_r, 1)
                if cur and nxt:
                    residual(pool, i, q)
                if nx2:
                    rstd(i + 2, mv1, nm1, ve1, rs1, bn1, r1l, r1, xn_r)
                if isinstance(i, int) and i == B - 1:
                    second_rstd(i - 1)
                    pool.wait_ge(scat, 16 + (i - 2) * 128)
                    scatter(i - 2, q, 0, SPLIT)
                    second_rstd(i)
                    scatter(i - 2, q, SPLIT)
                elif old:
                    scatter(i - 2, q)

            pool.wait_ge(c_ld, 16)
            rstd(0, mv1, nm1, ve1, rs1, bn1, r1l, r1, xn_r)
            pool.wait_ge(a_ld, 16)
            steps(pool, step, -1, B + 1, 2, B - 3)

            pool.wait_ge(tab_r, 1)
            pool.wait_ge(x1_st, 16 * B)

            pool.wait_ge(scat, 16 + 128 * (B - 2))
            for s in scat_end:
                pool.wait_ge(s, 128)

            def expert(e, half, more, full, tail, g0):
                hold(pool, pad_st, e * 16 + 16)
                with pool.Fori(0, full + tail) as k:
                    g = g0 + k
                    pool.dma_start(meta[:, :, :], xg[bass.ds(e * CAP + k * BLK, BLK), D:RW].rearrange("(t p) d -> p t d", t=NT))\
                        .then_inc(mt_ld, 16)
                    hold(pool, mt_ld, g * 16 + 16)
                    for t in range(NT):
                        pool.indirect_dma_start(gbr[:, t, :], None, gbscr,
                                                bass.IndirectOffsetOnAxis(ap=meta[:, t, E + 1:E + 2].bitcast(I32), axis=0))\
                            .then_inc(gb_ld, 16)
                    hold(pool, y_r, g + 2)
                    for t in range(NT):
                        pool.indirect_dma_start(out, bass.IndirectOffsetOnAxis(ap=meta[:, t, E:E + 1].bitcast(I32), axis=0),
                                                ysb[:, t, :], None, bounds_check=B * S - 1, oob_is_err=False,
                                                compute_op=ALU.add).then_inc(add_st, 16)
                    hold(pool, add_st, g * 32 + 32)

            experts(pool, tab, expert)


_ORDER = ["x", "wmc", "wmb", "attp", "cst", "we"]


def _halves(a):
    return a.reshape(KH, P, -1).transpose(1, 0, 2).reshape(P, -1)


def kernel(L0_attn_x, L0_attn_Wqkv_w, L0_attn_Wqkv_b, L0_attn_gn_w, L0_attn_gn_b, L0_attn_out_w, L0_attn_out_b,
           L0_ffn_gate_w, L0_ffn_w1, L0_ffn_w2, L0_ffn_w3, L0_c, L0_wmod):
    import concourse.bacc as bacc
    from concourse.bass_utils import run_bass_kernel_spmd as run

    a = {k: np.asarray(v) for k, v in locals().items() if k.startswith("L0")}

    def rows_of(v):
        return np.broadcast_to(v, (P, v.shape[0]))

    wqkv_b = a["L0_attn_Wqkv_b"]
    modc = {"cT": _halves(a["L0_c"].T), "wmodc": _halves(a["L0_wmod"][:, :2 * D])}
    modb = {"ob": rows_of(a["L0_attn_out_b"]), "wmodb": _halves(a["L0_wmod"][:, 2 * D:])}
    attp = {
        "wqkv": _halves(a["L0_attn_Wqkv_w"].T), "bkv": rows_of(wqkv_b[D:]), "ow": _halves(a["L0_attn_out_w"].T),
        "gate": _halves(a["L0_ffn_gate_w"].T), "bq": _halves(wqkv_b[:D, None]),
        "gnw": _halves(a["L0_attn_gn_w"][:, None]), "gnb": _halves(a["L0_attn_gn_b"][:, None]),
    }
    up = [a[n].transpose(0, 2, 1).reshape(E, KH, P, F).transpose(0, 2, 1, 3).reshape(E, P, KH * F) for n in ("L0_ffn_w1", "L0_ffn_w3")]
    down = a["L0_ffn_w2"].transpose(0, 2, 1).reshape(E, NF, P, D).transpose(0, 2, 1, 3).reshape(E, P, NF * D)
    arrays = {
        "x": a["L0_attn_x"].reshape(B * S, D),
        "wmc": np.concatenate([modc[n] for n in MODC], 1),
        "wmb": np.concatenate([modb[n] for n in MODB], 1),
        "attp": np.concatenate([attp[n] for n in ATTP], 1),
        "cst": constants()[0],
        "we": np.concatenate(up + [down], 2),
    }
    arrays = {k: np.ascontiguousarray(v) for k, v in arrays.items()}
    nc = bacc.Bacc("TRN2", target_bir_lowering=False, num_devices=1)
    args = [nc.dram_tensor(k, arrays[k].shape, F32, kind="ExternalInput").ap() for k in _ORDER]
    out = nc.dram_tensor("out", (B * S, D), F32, kind="ExternalOutput").ap()
    adaln_moe_kernel(nc, *args, out)
    r = run(nc, [arrays], core_ids=[0])
    return r.results[0]["out"].reshape(B, S, D)
```
